# Optimizing a Trainium2 kernel written in Bass

```python
import numpy as np
import jax
import jax.numpy as jnp

def _softmax(x, axis=-1):
    return jax.nn.softmax(x, axis=axis)

def _gelu(x):
    return jax.nn.gelu(x, approximate=True)

def _silu(x):
    return jax.nn.silu(x)

def _sigmoid(x):
    return jax.nn.sigmoid(x)

def _layernorm(x, axis=-1, eps=1e-05):
    m = jnp.mean(x, axis=axis, keepdims=True)
    v = jnp.var(x, axis=axis, keepdims=True)
    return (x - m) / jnp.sqrt(v + eps)

def _scatter_add(tgt, idx, src, axis=0):
    return tgt.at[idx].add(src)

def _segment_sum(src, seg, n):
    return jax.ops.segment_sum(src, seg, n)
kernel_name = 'mk_seq_preln_d1_jaxref_r4_16c52b'

def setup_inputs(seed: int=0):
    np.random.seed(seed)
    _w = jnp.asarray

    def _L0_attn_setup():
        import jax, jax.numpy as jnp
        import numpy as np
        B, N, D = (2, 512, 256)
        H, DH = (16, 64)
        SOFTCLAMP = 50.0
        SCALE = DH ** (-0.5)
        key = jax.random.key(seed)
        ks = jax.random.split(key, 5)
        std = D ** (-0.5)
        return {'x': jax.random.normal(ks[0], (B, N, D), dtype=jnp.float32), 'Wq': jax.random.normal(ks[1], (H * DH, D), dtype=jnp.float32) * std, 'Wk': jax.random.normal(ks[2], (H * DH, D), dtype=jnp.float32) * std, 'Wv': jax.random.normal(ks[3], (H * DH, D), dtype=jnp.float32) * std, 'Wo': jax.random.normal(ks[4], (D, H * DH), dtype=jnp.float32) * std}
    _L0_attn_in = _L0_attn_setup()

    def _L0_ffn_setup():
        import jax, jax.numpy as jnp
        import numpy as np
        D, FF, E, K = (256, 256, 8, 2)
        B, S = (4, 256)

        def _gelu(x):
            return jax.nn.gelu(x, approximate=False)
        key = jax.random.key(seed)
        ks = jax.random.split(key, 12)
        s = 0.02
        return {'x': jax.random.normal(ks[0], (B, S, D), jnp.float32), 'gate_w': jax.random.normal(ks[1], (D, E), jnp.float32) * s, 'gate_b': jnp.zeros((E,), jnp.float32), 'sw1': jax.random.normal(ks[2], (D, FF), jnp.float32) * s, 'sb1': jnp.zeros((FF,), jnp.float32), 'sw2': jax.random.normal(ks[3], (FF, D), jnp.float32) * s, 'sb2': jnp.zeros((D,), jnp.float32), 'w1': jax.random.normal(ks[4], (E, D, FF), jnp.float32) * s, 'b1': jnp.zeros((E, FF), jnp.float32), 'w2': jax.random.normal(ks[5], (E, FF, D), jnp.float32) * s, 'b2': jnp.zeros((E, D), jnp.float32)}
    _L0_ffn_in = _L0_ffn_setup()
    _d = {'L0_attn_x': _L0_attn_in['x'], 'L0_attn_Wq': _L0_attn_in['Wq'], 'L0_attn_Wk': _L0_attn_in['Wk'], 'L0_attn_Wv': _L0_attn_in['Wv'], 'L0_attn_Wo': _L0_attn_in['Wo'], 'L0_ffn_gate_w': _L0_ffn_in['gate_w'], 'L0_ffn_gate_b': _L0_ffn_in['gate_b'], 'L0_ffn_sw1': _L0_ffn_in['sw1'], 'L0_ffn_sb1': _L0_ffn_in['sb1'], 'L0_ffn_sw2': _L0_ffn_in['sw2'], 'L0_ffn_sb2': _L0_ffn_in['sb2'], 'L0_ffn_w1': _L0_ffn_in['w1'], 'L0_ffn_b1': _L0_ffn_in['b1'], 'L0_ffn_w2': _L0_ffn_in['w2'], 'L0_ffn_b2': _L0_ffn_in['b2']}
    _x0 = _d['L0_attn_x']
    _d['L0_attn_x'] = jax.random.normal(jax.random.fold_in(jax.random.key(seed), 1), (16, 512, 256), dtype=_x0.dtype)
    del _x0
    return _d

def reference(L0_attn_x, L0_attn_Wq, L0_attn_Wk, L0_attn_Wv, L0_attn_Wo, L0_ffn_gate_w, L0_ffn_gate_b, L0_ffn_sw1, L0_ffn_sb1, L0_ffn_sw2, L0_ffn_sb2, L0_ffn_w1, L0_ffn_b1, L0_ffn_w2, L0_ffn_b2):

    def _L0_attn_ref(x, Wq, Wk, Wv, Wo):
        import jax, jax.numpy as jnp
        import numpy as np
        B, N, D = (2, 512, 256)
        H, DH = (16, 64)
        SOFTCLAMP = 50.0
        SCALE = DH ** (-0.5)
        b, n, _ = x.shape
        q = jnp.einsum('bnd,fd->bnf', x, Wq).reshape(b, n, H, DH).transpose(0, 2, 1, 3)
        k = jnp.einsum('bnd,fd->bnf', x, Wk).reshape(b, n, H, DH).transpose(0, 2, 1, 3)
        v = jnp.einsum('bnd,fd->bnf', x, Wv).reshape(b, n, H, DH).transpose(0, 2, 1, 3)
        sim = jnp.einsum('bhid,bhjd->bhij', q, k) * SCALE
        sim = SOFTCLAMP * jnp.tanh(sim / SOFTCLAMP)
        causal = jnp.tril(jnp.ones((n, n), dtype=bool))
        sim = jnp.where(causal, sim, jnp.finfo(sim.dtype).min)
        attn = jax.nn.softmax(sim, axis=-1)
        out = jnp.einsum('bhij,bhjd->bhid', attn, v)
        out = out.transpose(0, 2, 1, 3).reshape(b, n, H * DH)
        return jnp.einsum('bnf,df->bnd', out, Wo)

    def _L0_ffn_ref(x, gate_w, gate_b, sw1, sb1, sw2, sb2, w1, b1, w2, b2):
        import jax, jax.numpy as jnp
        import numpy as np
        D, FF, E, K = (256, 256, 8, 2)
        B, S = (4, 256)

        def _gelu(x):
            return jax.nn.gelu(x, approximate=False)
        Bb, Ss, Dm = x.shape
        t = x.reshape(-1, Dm)
        T = t.shape[0]
        shared = _gelu(t @ sw1 + sb1) @ sw2 + sb2
        probs = jax.nn.softmax(t @ gate_w + gate_b, axis=-1)
        topk_p, topk_i = jax.lax.top_k(probs, K)
        combine = jnp.zeros((T, E), t.dtype).at[jnp.arange(T)[:, None], topk_i].set(topk_p)
        h = _gelu(jnp.einsum('td,edf->etf', t, w1) + b1[:, None, :])
        y = jnp.einsum('etf,efd->etd', h, w2) + b2[:, None, :]
        routed = jnp.einsum('te,etd->td', combine, y)
        return (routed + shared).reshape(Bb, Ss, Dm)
    x = L0_attn_x
    x = x + _L0_attn_ref(_layernorm(x, axis=-1), L0_attn_Wq, L0_attn_Wk, L0_attn_Wv, L0_attn_Wo)
    x = x + _L0_ffn_ref(_layernorm(x, axis=-1), L0_ffn_gate_w, L0_ffn_gate_b, L0_ffn_sw1, L0_ffn_sb1, L0_ffn_sw2, L0_ffn_sb2, L0_ffn_w1, L0_ffn_b1, L0_ffn_w2, L0_ffn_b2)
    return x

_drawn_inputs = setup_inputs


def setup_inputs(seed=0):
    import zlib

    import numpy as np

    out = dict(_drawn_inputs(seed))
    spreads = {'L0_ffn_gate_b': (0.0, 0.521),
     'L0_ffn_sb1': (0.0, 0.536),
     'L0_ffn_sb2': (0.0, 0.1),
     'L0_ffn_b1': (0.0, 0.8),
     'L0_ffn_b2': (0.0, 0.332)}
    factors = {'L0_ffn_w1': 4.301, 'L0_ffn_w2': 4.011}
    for name, (base, spread) in spreads.items():
        noise = np.random.default_rng([zlib.crc32(name.encode()), seed]).standard_normal(out[name].shape)
        drawn = base * np.exp(spread * noise) if base else spread * noise
        out[name] = jnp.asarray(drawn.astype(out[name].dtype))
    for name, factor in factors.items():
        out[name] = (out[name] * factor).astype(out[name].dtype)
    return out
```

```python
from contextlib import ExitStack

import concourse.bass as bass
from concourse import mybir

F32 = mybir.dt.float32
F32R = mybir.dt.float32r
I32 = mybir.dt.int32
ALU = mybir.AluOpType
ACT = mybir.ActivationFunctionType
AX = mybir.AxisListType

P = 128
D = 256
DC = D // P
NSEQ, N = 16, 512
NT = N // P
H, DH = 16, 64
PAIRS = H // 2
HD = H * DH
HALF = HD // 2
FF = 256
FC = FF // P
E = 8
NE = E + 1
SOFTCLAMP = 50.0
SCALE = DH ** -0.5
EPS = 1e-5
RSQRT_GUESS = float(0x5F3759DF)
NEWTON = 3
LN_STEPS = 4 + 3 * NEWTON

SCORE_UNITS = [[(0, 0)], [(1, 0), (3, N - P)], [(2, 0)]]
UNIT_COLS = [N, N, N // 2]
UNIT_AT = [0, 2 * N, 4 * N]
PROB_COLS = 5 * N


def ring_plan():
    units = []
    for p in range(PAIRS):
        units += [("scores", p, u) for u in range(3)]
        if p + 1 < PAIRS:
            units.append(("qk", p + 1, 0))
        else:
            units.append(("turn1", 0, 0))
        if p == PAIRS // 2:
            units += [("v", 1, 0), ("v", 1, 1)]
    units += [("qk", 0, 0), ("v", 0, 0), ("v", 0, 1), ("turn2", 0, 0), ("gate", 0, 0)]
    units += [("hidden", e, 0) for e in range(NE)]
    return units


RING = ring_plan()
EMPTIED_BY_ACT = ("scores", "v", "hidden")
RING_FIRST = 4
ACT_FIRST = DVE_FIRST = 2
ACT_TURN = sum(k[0] in EMPTIED_BY_ACT for k in RING)
DVE_TURN = len(RING) - ACT_TURN
assert len(RING) % 2 == 0 and RING_FIRST % 2 == 0


def emptied(n):
    by_act = sum(k[0] in EMPTIED_BY_ACT for k in RING[:n + 1])
    return by_act, n + 1 - by_act


def block_program(nc, x, wqT, wkT, wvT, woT, gate_w, gate_b_rows, w1s, w1, w2s, w2,
                  b1_cols, b2_twice, sb2_cols, out):
    with ExitStack() as ctx:
        def sb(name, shape, dt=F32, stack=ctx):
            return stack.enter_context(nc.sbuf_tensor(name, shape, dt))

        def ps(name, shape):
            return ctx.enter_context(nc.psum_tensor(name, shape, F32))

        def sem(name):
            return ctx.enter_context(nc.semaphore(name))

        w_qk = [sb(f"w_qk{s}", [P, 2, DC, HD], F32R) for s in ("h", "l")]
        w_v = [sb(f"w_v{s}", [P, DC, HD], F32R) for s in ("h", "l")]
        w_o = [sb(f"w_o{s}", [P, PAIRS, D], F32R) for s in ("h", "l")]
        w_1 = [sb(f"w_1{s}", [P, NE, DC, FF], F32R) for s in ("h", "l")]
        w_2 = [sb(f"w_2{s}", [P, NE, FC, D], F32R) for s in ("h", "l")]
        w_g = [sb(f"w_g{s}", [P, DC, E], F32R) for s in ("h", "l")]
        b_2 = [sb(f"b_2{s}", [2 * E, D], F32R) for s in ("h", "l")]
        pick = sb("pick", [2 * E, E, P], F32R)
        b1c = sb("b1c", [P, NE, FC])
        sb2c = sb("sb2c", [P, DC])
        gate_b = sb("gate_b", [P, E])
        ident = sb("ident", [P, P])
        ones = sb("ones", [P, DH])
        lower = sb("lower", [P, E, E])

        x_next = sb("x_next", [P, NT, D])
        x_res = sb("x_res", [P, NT, D])
        xnT = [sb(f"xnT{s}", [P, DC, N], F32R) for s in ("h", "l")]
        qkT = [sb(f"qkT{s}", [P, 2, N], F32R) for s in ("h", "l")]
        v = sb("v", [P, NT, HALF])
        stats = sb("stats", [P, NT, 6])
        mean_var = sb("mean_var", [P, NT, 2])
        var_eps = sb("var_eps", [P, NT, 1])
        minus_half = sb("minus_half", [P, NT, 1])
        rstd = sb("rstd", [P, NT, 1])
        newton = sb("newton", [P, NT, 1])
        logit = sb("logit", [P, NT, E])
        row1 = sb("row1", [P, NT, 1])
        prob8 = sb("prob8", [P, NT, E])
        combine = sb("combine", [P, NT, E])
        combine2 = sb("combine2", [P, NT, 2 * E], F32R)

        with ExitStack() as arena:
            prob = [sb(f"prob{k}", [P, PROB_COLS], F32, arena) for k in range(2)]
            key_sum = sb("key_sum", [P, 2, N - P], F32, arena)
            recip = sb("recip", [P, N], F32, arena)
            o_norm = sb("o_norm", [P, N], F32, arena)
            oT = [sb(f"oT{s}", [P, N], F32R, arena) for s in ("h", "l")]
        with ExitStack() as arena:
            attnT = sb("attnT", [P, DC, N], F32, arena)
        with ExitStack() as arena:
            hT = [[sb(f"hT{k}{s}", [P, FC, N], F32R, arena) for s in ("h", "l")] for k in range(2)]
            gelu = sb("gelu", [P, FC, N], F32, arena)
            x2T = [sb(f"x2T{s}", [P, DC, N], F32R, arena) for s in ("h", "l")]
            combineT = sb("combineT", [2 * E, N], F32R, arena)
        with ExitStack() as arena:
            sb("under_yT", [P, 4 * N], F32, arena)
            yT = sb("yT", [P, DC, N], F32, arena)
        with ExitStack() as arena:
            stage = [sb(f"stage{k}", [P, 2048], F32, arena) for k in range(3)]
            small = sb("small", [P, DC * E], F32, arena)
            small2 = sb("small2", [2 * E, D], F32, arena)
            pick_f = sb("pick_f", [2 * E, E, P], F32, arena)
        with ExitStack() as arena:
            sb("under_compare", [P, 4 * N], F32, arena)
            greater = sb("greater", [P, NT, E, E], F32, arena)
            equal = sb("equal", [P, NT, E, E], F32, arena)

        ring = [ps(f"ring{k}", [P, 2, N]) for k in range(2)]
        acc = ps("acc", [P, 2, N])
        bank_o = ps("bank_o", [P, N])
        bank_d = ps("bank_d", [P, N])

        small_loaded = sem("small_loaded")
        stage_loaded = [sem(f"stage_loaded{k}") for k in range(3)]
        hi_split = sem("hi_split")
        lo_split = sem("lo_split")
        const_ready = sem("const_ready")
        xnext_loaded = sem("xnext_loaded")
        xres_loaded = sem("xres_loaded")
        stored = sem("stored")
        ring_full = sem("ring_full")
        act_emptied = sem("act_emptied")
        dve_emptied = sem("dve_emptied")
        turn_hi = sem("turn_hi")
        exp_done = sem("exp_done")
        masked = sem("masked")
        sum_steps = sem("sum_steps")
        den_done = sem("den_done")
        o_steps = sem("o_steps")
        attn_done = sem("attn_done")
        attn_copied = sem("attn_copied")
        turned_attn = sem("turned_attn")
        x1_ready = sem("x1_ready")
        ln_steps = sem("ln_steps")
        xn_ready = sem("xn_ready")
        gate_steps = sem("gate_steps")
        gate_exp = sem("gate_exp")
        turned_gate = sem("turned_gate")
        combine_ready = sem("combine_ready")
        spread = sem("spread")
        h_steps = sem("h_steps")
        y_done = sem("y_done")
        acc_done = sem("acc_done")
        y_copied = sem("y_copied")
        turned_y = sem("turned_y")
        out_ready = sem("out_ready")

        pieces = [
            ([(wqT.rearrange("(c p) f -> p c f", p=P), 0, 2048)], [w[:, 0] for w in w_qk], (DC, HD)),
            ([(wkT.rearrange("(c p) f -> p c f", p=P), 0, 2048)], [w[:, 1] for w in w_qk], (DC, HD)),
            ([(wvT.rearrange("(c p) f -> p c f", p=P), 0, 2048)], [w[:, :] for w in w_v], (DC, HD)),
            ([(woT.rearrange("(k p) d -> p k d", p=P), 0, 2048)], [w[:, :] for w in w_o], (PAIRS, D)),
        ]
        for shared, routed, dst in ((w1s, w1, w_1), (w2s, w2, w_2)):
            one = DC * FF
            pieces.append((
                [(shared.rearrange("(c p) f -> p c f", p=P), 0, one),
                 (routed[0:2].rearrange("e (c p) f -> p (e c) f", p=P), one, 3 * one)],
                [w[:, 0:3].rearrange("p e c f -> p (e c) f") for w in dst], (3 * DC, FF)))
            for e0 in (2, 5):
                pieces.append((
                    [(routed[e0:e0 + 3].rearrange("e (c p) f -> p (e c) f", p=P), 0, 3 * one)],
                    [w[:, e0 + 1:e0 + 4].rearrange("p e c f -> p (e c) f") for w in dst], (3 * DC, FF)))
        NPIECES = len(pieces)
        NPARTS = [0, 0, 0]
        piece_loaded = []
        for k, (srcs, _, _) in enumerate(pieces):
            NPARTS[k % 3] += len(srcs)
            piece_loaded.append(16 * NPARTS[k % 3])

        def staged(k):
            (a, b) = pieces[k][2]
            return stage[k % 3][:, 0:a * b].rearrange("p (a b) -> p a b", a=a)

        x_tiles = x.rearrange("s (t p) d -> s p t d", p=P)
        out_tiles = out.rearrange("s (t p) d -> s p t d", p=P)
        

        block = ctx.enter_context(nc.Block())

        @block.sync
        def _(sp):
            sp.dma_start(x_next[:, :, :], x_tiles[0]).then_inc(xnext_loaded, 16)
            for k, (srcs, _, _) in enumerate(pieces):
                if k == 3:
                    sp.dma_start(small[:, :], gate_w.rearrange("(c p) e -> p c e", p=P)).then_inc(small_loaded, 16)
                    sp.dma_start(small2[:, :], b2_twice).then_inc(small_loaded, 16)
                    sp.dma_start(b1c[:, :, :], b1_cols).then_inc(small_loaded, 16)
                    sp.dma_start(sb2c[:, :], sb2_cols).then_inc(small_loaded, 16)
                    sp.dma_start(gate_b[:, :], gate_b_rows).then_inc(small_loaded, 16)
                if k >= 3:
                    sp.wait_ge(lo_split, k - 2)
                for src, a, b in srcs:
                    dst = stage[k % 3][:, a:b].rearrange("p (a b) -> p a b", b=src.shape[2])
                    sp.dma_start(dst, src).then_inc(stage_loaded[k % 3], 16)
            sp.wait_ge(ring_full, 1)
            with sp.Fori(0, NSEQ) as i:
                sp.dma_start(x_next[:, :, :], x_tiles[(i + 1) % NSEQ]).then_inc(xnext_loaded, 16)
                sp.wait_ge(xnext_loaded, 16)
                sp.wait_ge(out_ready, i + 1)
                sp.dma_start(x_res[:, :, :], x_tiles[i]).then_inc(xres_loaded, 16)
                sp.wait_ge(out_ready, i + 2)
                sp.dma_start(out_tiles[i], x_next[:, :, :]).then_inc(stored, 16)
                stores = sp.to_reg(i * 16 + 16)
                sp.wait_ge(xnext_loaded, 16)
                sp.wait_ge(stored, stores)

        @block.gpsimd
        def _(pool):
            nc.gpsimd.memset(ident[:, :], 0.0)
            nc.gpsimd.memset(ones[:, :], 1.0)
            nc.gpsimd.memset(lower[:, :, :], 1.0)
            nc.gpsimd.memset(pick_f[:, :, :], 0.0).then_inc(const_ready, 1)
            pool.wait_ge(const_ready, 1)
            nc.gpsimd.affine_select(out=ident[:, :], in_=ident[:, :], compare_op=ALU.not_equal, fill=1.0,
                                    base=0, pattern=[[-1, P]], channel_multiplier=1)
            nc.gpsimd.affine_select(out=lower[:, :, :], in_=lower[:, :, :], compare_op=ALU.is_gt, fill=0.0,
                                    base=0, pattern=[[1, E], [-1, E]], channel_multiplier=0)
            nc.gpsimd.affine_select(out=pick_f[:, :, :], in_=pick_f[:, :, :], compare_op=ALU.not_equal,
                                    fill=1.0, base=0, pattern=[[-1, E], [0, P]],
                                    channel_multiplier=1).then_inc(const_ready, 1)
            pool.wait_ge(const_ready, 2)
            nc.gpsimd.affine_select(out=pick_f[:, :, :], in_=pick_f[:, :, :], compare_op=ALU.not_equal,
                                    fill=1.0, base=-E, pattern=[[-1, E], [0, P]],
                                    channel_multiplier=1).then_inc(const_ready, 1)

            with pool.Fori(0, NSEQ) as i:
                for p in range(PAIRS):
                    pb = prob[p % 2]
                    for u in range(3):
                        w = UNIT_COLS[u]
                        tiles = pb[:, UNIT_AT[u]:UNIT_AT[u] + 2 * w].rearrange("p (h q) -> p h q", h=2)
                        exps = pool.to_reg(i * 24 + (3 * p + u + 1))
                        pool.wait_ge(const_ready, 3)
                        pool.wait_ge(exp_done, exps)
                        for _, at in SCORE_UNITS[u]:
                            diag = tiles[:, :, at:at + P]
                            last = nc.gpsimd.affine_select(out=diag, in_=diag, compare_op=ALU.is_ge, fill=0.0,
                                                           base=0, pattern=[[0, 2], [1, P]],
                                                           channel_multiplier=-1)
                        last.then_inc(masked, 1)
                    t0 = pb[:, 0:2 * N].rearrange("p (h q) -> p h q", h=2)
                    t13 = pb[:, 2 * N:4 * N].rearrange("p (h q) -> p h q", h=2)
                    t2 = pb[:, 4 * N:5 * N].rearrange("p (h q) -> p h q", h=2)
                    pool.wait_ge(masked, i * 24 + 3 * p + 3)
                    if p >= 1:
                        pool.wait_ge(den_done, i * 8 + p)
                    nc.gpsimd.tensor_tensor(key_sum[:, :, :], t0[:, :, P:N], t13[:, :, 0:N - P],
                                            ALU.add).then_inc(sum_steps, 1)
                    pool.wait_ge(sum_steps, i * 24 + 3 * p + 1)
                    nc.gpsimd.tensor_tensor(key_sum[:, :, P:], key_sum[:, :, P:], t2[:, :, :],
                                            ALU.add).then_inc(sum_steps, 1)
                    pool.wait_ge(sum_steps, i * 24 + 3 * p + 2)
                    nc.gpsimd.tensor_tensor(key_sum[:, :, 2 * P:], key_sum[:, :, 2 * P:], t13[:, :, N - P:],
                                            ALU.add).then_inc(sum_steps, 1)

        @block.scalar
        def _(act):
            def split_hi(k):
                act.wait_ge(stage_loaded[k % 3], piece_loaded[k])
                nc.scalar.copy(pieces[k][1][0], staged(k)).then_inc(hi_split, 1)

            for k in range(3):
                split_hi(k)

            def copy_v(slot, part, full):
                act.wait_ge(ring_full, full)
                nc.scalar.copy(v[:, 2 * part:2 * part + 2, :], slot[:, :, :]).then_inc(act_emptied, 1)

            for k in range(3, NPIECES):
                split_hi(k)
            for part in range(2):
                copy_v(ring[part], part, 3 + part)
            act.wait_ge(lo_split, NPIECES)
            with act.Fori(0, NSEQ) as i:
                def full(n):
                    return i * len(RING) + (RING_FIRST + n + 1)

                def exponentiate(n):
                    _, p, u = RING[n]
                    cols = prob[p % 2][:, UNIT_AT[u]:UNIT_AT[u] + 2 * UNIT_COLS[u]]
                    act.wait_ge(act_emptied, i * ACT_TURN + (ACT_FIRST + emptied(n)[0]))
                    nc.scalar.activation(cols, cols, ACT.Exp, scale=SOFTCLAMP).then_inc(exp_done, 1)

                waiting = None
                for n, (kind, a, b) in enumerate(RING):
                    slot = ring[n % 2]
                    if kind == "scores":
                        p, u = a, b
                        w = UNIT_COLS[u]
                        if u == 0 and p >= 2:
                            act.wait_ge(den_done, i * 8 + (p - 1))
                        act.wait_ge(ring_full, full(n))
                        dst = prob[p % 2][:, UNIT_AT[u]:UNIT_AT[u] + 2 * w]
                        nc.scalar.activation(dst.rearrange("p (h q) -> p h q", h=2), slot[:, :, 0:w],
                                             ACT.Tanh, scale=SCALE / SOFTCLAMP).then_inc(act_emptied, 1)
                        if waiting is not None:
                            exponentiate(waiting)
                        waiting = n
                    elif waiting is not None and kind in ("v", "turn1"):
                        exponentiate(waiting)
                        waiting = None
                    if kind == "v":
                        copy_v(slot, b, full(n))
                        if a == 0 and b == 1:
                            act.wait_ge(attn_done, i + 1)
                            nc.scalar.copy(attnT[:, 0, :], acc[:, 0, :]).then_inc(attn_copied, 1)
                            act.wait_ge(gate_steps, i * 12 + 4)
                            nc.scalar.activation(logit[:, :, :], logit[:, :, :], ACT.Exp).then_inc(gate_exp, 1)
                    if kind == "hidden":
                        e = a
                        act.wait_ge(ring_full, full(n))
                        if e >= 1:
                            act.wait_ge(h_steps, i * 26 + (3 * e - 1))
                        for c in range(FC):
                            last = nc.scalar.activation(gelu[:, c, :], slot[:, c, :], ACT.Gelu,
                                                        bias=b1c[:, e, c:c + 1])
                        last.then_inc(act_emptied, 1)
                act.wait_ge(acc_done, i * 2 + 1)
                nc.scalar.activation(yT[:, 0, :], acc[:, 0, :], ACT.Identity,
                                     bias=sb2c[:, 0:1]).then_inc(y_copied, 1)

        @block.vector
        def _(dve):
            def split_lo(k):
                dve.wait_ge(hi_split, k + 1)
                nc.vector.tensor_tensor(pieces[k][1][1], staged(k), pieces[k][1][0].bitcast(F32),
                                        ALU.subtract).then_inc(lo_split, 1)

            def layernorm_stats(src, steps):
                for t in range(NT):
                    last = nc.vector.bn_stats(stats[:, t, :], src[:, t, :])
                last.then_inc(ln_steps, 1)
                stats_done = dve.to_reg(steps + 1)
                dve.wait_ge(xnext_loaded, 16)
                dve.wait_ge(ln_steps, stats_done)
                for t in range(NT):
                    last = nc.vector.bn_aggr(mean_var[:, t, :], stats[:, t, :])
                last.then_inc(ln_steps, 1)
                dve.wait_ge(ln_steps, steps + 2)
                nc.vector.tensor_scalar(var_eps[:, :, :], mean_var[:, :, 1:2], EPS, None, ALU.add)
                nc.vector.tensor_scalar(minus_half[:, :, :], mean_var[:, :, 1:2], EPS, -0.5, ALU.add,
                                        ALU.mult).then_inc(ln_steps, 1)
                dve.wait_ge(ln_steps, steps + 3)
                nc.vector.tensor_scalar(rstd[:, :, :].bitcast(I32), var_eps[:, :, :].bitcast(I32), -0.5,
                                        RSQRT_GUESS, ALU.mult, ALU.add).then_inc(ln_steps, 1)
                for k in range(NEWTON):
                    dve.wait_ge(ln_steps, steps + (4 + 3 * k))
                    nc.vector.tensor_tensor(newton[:, :, :], rstd[:, :, :], rstd[:, :, :],
                                            ALU.mult).then_inc(ln_steps, 1)
                    dve.wait_ge(ln_steps, steps + (5 + 3 * k))
                    nc.vector.tensor_tensor(newton[:, :, :], newton[:, :, :], minus_half[:, :, :],
                                            ALU.mult).then_inc(ln_steps, 1)
                    dve.wait_ge(ln_steps, steps + (6 + 3 * k))
                    nc.vector.scalar_tensor_tensor(rstd[:, :, :], newton[:, :, :], 1.5, rstd[:, :, :],
                                                   ALU.add, ALU.mult).then_inc(ln_steps, 1)

            def layernorm_apply(src, steps):
                dve.wait_ge(ln_steps, steps + LN_STEPS)
                for t in range(NT):
                    last = nc.vector.tensor_scalar(x_next[:, t, :], src[:, t, :], mean_var[:, t, 0:1],
                                                   rstd[:, t, :], ALU.subtract, ALU.mult)
                last.then_inc(xn_ready, 1)

            def empty_split(dst, slot, full, his):
                dve.wait_ge(ring_full, full)
                nc.vector.tensor_copy(dst[0][:, :, :], slot[:, :, :]).then_inc(turn_hi, 1)
                dve.wait_ge(turn_hi, his)
                nc.vector.tensor_tensor(dst[1][:, :, :], slot[:, :, :], dst[0][:, :, :].bitcast(F32),
                                        ALU.subtract).then_inc(dve_emptied, 1)

            dve.wait_ge(xnext_loaded, 16)
            layernorm_stats(x_next, 0)
            layernorm_apply(x_next, 0)
            for k in range(2):
                split_lo(k)
            dve.wait_ge(const_ready, 3)
            nc.vector.tensor_copy(pick[:, :, :], pick_f[:, :, :]).then_inc(out_ready, 1)
            empty_split(xnT, ring[0], 1, 1)
            split_lo(2)
            empty_split(qkT, ring[1], 2, 2)
            dve.wait_ge(small_loaded, 16 * 5)
            g3 = small[:, :].rearrange("p (c e) -> p c e", c=DC)
            nc.vector.tensor_copy(w_g[0][:, :, :], g3)
            nc.vector.tensor_copy(b_2[0][:, :], small2[:, :]).then_inc(gate_steps, 1)
            dve.wait_ge(gate_steps, 1)
            nc.vector.tensor_tensor(w_g[1][:, :, :], g3, w_g[0][:, :, :].bitcast(F32), ALU.subtract)
            nc.vector.tensor_tensor(b_2[1][:, :], small2[:, :], b_2[0][:, :].bitcast(F32),
                                    ALU.subtract).then_inc(gate_steps, 1)
            dve.wait_ge(gate_steps, 2)
            for k in range(3, NPIECES):
                split_lo(k)

            with dve.Fori(0, NSEQ) as i:
                def full(n):
                    return i * len(RING) + (RING_FIRST + n + 1)

                def his(n):
                    return i * (DVE_TURN - 1) + (DVE_FIRST + emptied(n)[1])

                def normalise(p):
                    dve.wait_ge(den_done, i * 8 + (p + 1))
                    nc.vector.reciprocal(recip[:, :], bank_d[:, :]).then_inc(o_steps, 1)
                    dve.wait_ge(o_steps, i * 32 + (4 * p + 1))
                    nc.vector.tensor_tensor(o_norm[:, :], bank_o[:, :], recip[:, :], ALU.mult).then_inc(o_steps, 1)
                    dve.wait_ge(o_steps, i * 32 + (4 * p + 2))
                    nc.vector.tensor_copy(oT[0][:, :], o_norm[:, :]).then_inc(o_steps, 1)
                    dve.wait_ge(o_steps, i * 32 + (4 * p + 3))
                    nc.vector.tensor_tensor(oT[1][:, :], o_norm[:, :], oT[0][:, :].bitcast(F32),
                                            ALU.subtract).then_inc(o_steps, 1)

                for p in range(PAIRS):
                    if p == 6:
                        layernorm_apply(x_next, i * (2 * LN_STEPS) + LN_STEPS)
                    if p + 1 < PAIRS:
                        n = RING.index(("qk", p + 1, 0))
                        empty_split(qkT, ring[n % 2], full(n), his(n))
                    else:
                        n = RING.index(("turn1", 0, 0))
                        empty_split(xnT, ring[n % 2], full(n), his(n))
                    if p >= 1:
                        normalise(p - 1)
                    if p == 5:
                        dve.wait_ge(xnext_loaded, i * 16 + 32)
                        layernorm_stats(x_next, i * (2 * LN_STEPS) + LN_STEPS)
                n = RING.index(("qk", 0, 0))
                empty_split(qkT, ring[n % 2], full(n), his(n))
                normalise(PAIRS - 1)

                dve.wait_ge(attn_done, i + 1)
                nc.vector.tensor_copy(attnT[:, 1, :], acc[:, 1, :]).then_inc(attn_copied, 1)
                dve.wait_ge(turned_attn, i + 1)
                dve.wait_ge(xres_loaded, i * 16 + 16)
                for k, bank in enumerate((bank_o, bank_d)):
                    half = x_res[:, 2 * k:2 * k + 2, :].rearrange("p t d -> p (t d)")
                    last = nc.vector.tensor_tensor(half, half, bank[:, :], ALU.add)
                last.then_inc(x1_ready, 1)
                dve.wait_ge(x1_ready, i + 1)
                layernorm_stats(x_res, i * (2 * LN_STEPS) + 2 * LN_STEPS)
                layernorm_apply(x_res, i * (2 * LN_STEPS) + 2 * LN_STEPS)
                n = RING.index(("turn2", 0, 0))
                empty_split(x2T, ring[n % 2], full(n), his(n))

                n = RING.index(("gate", 0, 0))
                gates = ring[n % 2][:, 0, 0:NT * E].rearrange("p (t e) -> p t e", t=NT)
                step = [0]

                def then(ins):
                    step[0] += 1
                    ins.then_inc(gate_steps, 1)
                    dve.wait_ge(gate_steps, i * 12 + (2 + step[0]))

                dve.wait_ge(ring_full, full(n))
                nc.vector.tensor_tensor(logit[:, :, :], gates, gate_b[:, None, :].to_broadcast([P, NT, E]),
                                        ALU.add).then_inc(dve_emptied, 1)
                dve.wait_ge(dve_emptied, i * DVE_TURN + (DVE_FIRST + emptied(n)[1]))
                then(nc.vector.tensor_reduce(row1[:, :, :], logit[:, :, :], AX.X, ALU.max))
                then(nc.vector.tensor_tensor(logit[:, :, :], logit[:, :, :],
                                             row1[:, :, :].to_broadcast([P, NT, E]), ALU.subtract))
                dve.wait_ge(gate_exp, i + 1)
                then(nc.vector.tensor_reduce(row1[:, :, :], logit[:, :, :], AX.X, ALU.add))
                then(nc.vector.reciprocal(row1[:, :, :], row1[:, :, :]))
                then(nc.vector.tensor_tensor(prob8[:, :, :], logit[:, :, :],
                                             row1[:, :, :].to_broadcast([P, NT, E]), ALU.mult))
                shape = [P, NT, E, E]
                other = prob8[:, :, None, :].to_broadcast(shape)
                own = prob8[:, :, :, None].to_broadcast(shape)
                nc.vector.tensor_tensor(greater[:, :, :, :], other, own, ALU.is_gt)
                then(nc.vector.tensor_tensor(equal[:, :, :, :], other, own, ALU.is_equal))
                then(nc.vector.tensor_tensor(equal[:, :, :, :], equal[:, :, :, :],
                                             lower[:, None, :, :].to_broadcast(shape), ALU.mult))
                then(nc.vector.tensor_tensor(greater[:, :, :, :], greater[:, :, :, :], equal[:, :, :, :],
                                             ALU.add))
                then(nc.vector.tensor_reduce(combine[:, :, :], greater[:, :, :, :], AX.X, ALU.add))
                then(nc.vector.scalar_tensor_tensor(combine[:, :, :], combine[:, :, :], 2.0, prob8[:, :, :],
                                                    ALU.is_lt, ALU.mult))
                then(nc.vector.tensor_copy(combine2[:, :, 0:E], combine[:, :, :]))
                then(nc.vector.tensor_tensor(combine2[:, :, E:], combine[:, :, :],
                                             combine2[:, :, 0:E].bitcast(F32), ALU.subtract))
                assert step[0] == 12
                dve.wait_ge(turned_gate, i + 1)
                nc.vector.tensor_copy(combineT[:, :], bank_d[0:2 * E, :]).then_inc(combine_ready, 1)

                for e in range(NE):
                    n = RING.index(("hidden", e, 0))
                    dve.wait_ge(act_emptied, i * ACT_TURN + (ACT_FIRST + emptied(n)[0]))
                    if e >= 1:
                        bank = bank_o if e % 2 else bank_d
                        dve.wait_ge(spread, i * 8 + e)
                        nc.vector.tensor_tensor(gelu[:, :, :], gelu[:, :, :],
                                                bank[:, None, :].to_broadcast([P, FC, N]),
                                                ALU.mult).then_inc(h_steps, 1)
                        dve.wait_ge(h_steps, i * 26 + 3 * e)
                    if e >= 2:
                        dve.wait_ge(y_done, i * 8 + (e - 1))
                    hh, hl = hT[e % 2]
                    nc.vector.tensor_copy(hh[:, :, :], gelu[:, :, :]).then_inc(h_steps, 1)
                    dve.wait_ge(h_steps, i * 26 + (3 * e + 1))
                    nc.vector.tensor_tensor(hl[:, :, :], gelu[:, :, :], hh[:, :, :].bitcast(F32),
                                            ALU.subtract).then_inc(h_steps, 1)

                dve.wait_ge(acc_done, i * 2 + 2)
                nc.vector.tensor_scalar(yT[:, 1, :], acc[:, 1, :], sb2c[:, 1:2], None,
                                        ALU.add).then_inc(y_copied, 1)
                dve.wait_ge(turned_y, i + 1)
                for k, bank in enumerate((bank_o, bank_d)):
                    half = slice(2 * k, 2 * k + 2)
                    last = nc.vector.tensor_tensor(x_next[:, half, :].rearrange("p t d -> p (t d)"),
                                                   x_res[:, half, :].rearrange("p t d -> p (t d)"),
                                                   bank[:, :], ALU.add)
                last.then_inc(out_ready, 1)

        @block.tensor
        def _(pe):
            def product(dst, w, m, start, stop):
                pe.matmul(dst, w[0], m[0], start=start, stop=False)
                pe.matmul(dst, w[0], m[1], start=False, stop=False)
                return pe.matmul(dst, w[1], m[0], start=False, stop=stop)

            def turn_tokens(slot, src):
                for c in range(DC):
                    for t in range(NT):
                        last = pe.transpose(slot[:, c, t * P:(t + 1) * P], src[:, t, c * P:(c + 1) * P],
                                            ident[:, :])
                last.then_inc(ring_full, 1)

            def project_qk(slot, p):
                for m in range(2):
                    for c in range(DC):
                        last = product(slot[:, m, :], [w[:, m, c, p * P:(p + 1) * P] for w in w_qk],
                                       [a[:, c, :] for a in xnT], c == 0, c == DC - 1)
                last.then_inc(ring_full, 1)

            def project_v(slot, half, part):
                for k in range(2):
                    t = 2 * part + k
                    for c in range(DC):
                        last = product(slot[:, k, :], [a[:, c, t * P:(t + 1) * P] for a in xnT],
                                       [w[:, c, half * HALF:(half + 1) * HALF] for w in w_v],
                                       c == 0, c == DC - 1)
                last.then_inc(ring_full, 1)

            pe.wait_ge(const_ready, 3)
            pe.wait_ge(xn_ready, 1)
            turn_tokens(ring[0], x_next)
            pe.wait_ge(lo_split, 2)
            pe.wait_ge(dve_emptied, 1)
            project_qk(ring[1], 0)
            pe.wait_ge(lo_split, 3)
            project_v(ring[0], 0, 0)
            pe.wait_ge(dve_emptied, 2)
            project_v(ring[1], 0, 1)
            pe.wait_ge(lo_split, NPIECES)
            pe.wait_ge(gate_steps, 2)

            with pe.Fori(0, NSEQ) as i:
                def acts(k):
                    return i * ACT_TURN + (ACT_FIRST + k)

                def dves(k):
                    return i * DVE_TURN + (DVE_FIRST + k)

                turn = [0]

                def slot_for(*unit):
                    n = turn[0]
                    assert RING[n] == unit
                    turn[0] += 1
                    if n < 2:
                        pe.wait_ge(act_emptied, acts(0))
                    elif RING[n - 2][0] in EMPTIED_BY_ACT:
                        pe.wait_ge(act_emptied, acts(emptied(n - 2)[0]))
                    else:
                        pe.wait_ge(dve_emptied, dves(emptied(n - 2)[1]))
                    return ring[n % 2]

                def scores(p, u):
                    slot = slot_for("scores", p, u)
                    if u == 0:
                        n = RING.index(("qk", p, 0)) if p else -1
                        pe.wait_ge(dve_emptied, dves(emptied(n)[1] if p else 0))
                    for j, at in SCORE_UNITS[u]:
                        q = slice(j * P, N)
                        for n, (a, b) in enumerate(((0, 0), (0, 1), (1, 0))):
                            for h in range(2):
                                r = slice(h * DH, (h + 1) * DH)
                                last = pe.matmul(slot[:, h, at:at + N - j * P],
                                                 qkT[a][r, 1, j * P:(j + 1) * P], qkT[b][r, 0, q],
                                                 start=(n == 0), stop=(n == 2))
                    last.then_inc(ring_full, 1)

                def values(p):
                    if p == 0:
                        pe.wait_ge(out_ready, i + 1)
                        pe.wait_ge(act_emptied, acts(0))
                    else:
                        pe.wait_ge(o_steps, i * 32 + (4 * p - 2))
                    if p == PAIRS // 2:
                        n = RING.index(("v", 1, 1))
                        pe.wait_ge(act_emptied, acts(emptied(n)[0]))
                    units = [(u, j, at) for u in range(3) for j, at in SCORE_UNITS[u]]
                    for k, (u, j, at) in enumerate(units):
                        pe.wait_ge(masked, i * 24 + (3 * p + u + 1))
                        for h in range(2):
                            f = (p % (PAIRS // 2)) * P + h * DH
                            a = UNIT_AT[u] + h * UNIT_COLS[u] + at
                            pe.matmul(bank_o[h * DH:(h + 1) * DH, j * P:N], v[:, j, f:f + DH],
                                      prob[p % 2][:, a:a + N - j * P],
                                      start=(k == 0), stop=(k == len(units) - 1))

                def denominators(p):
                    pe.wait_ge(sum_steps, i * 24 + (3 * p + 3))
                    for h in range(2):
                        pe.matmul(bank_d[h * DH:(h + 1) * DH, 0:P], ones[:, :],
                                  prob[p % 2][:, h * N:h * N + P], start=True, stop=True)
                    for h in range(2):
                        last = pe.matmul(bank_d[h * DH:(h + 1) * DH, P:N], ones[:, :], key_sum[:, h, :],
                                         start=True, stop=True)
                    last.then_inc(den_done, 1)

                def project_out(p):
                    pe.wait_ge(o_steps, i * 32 + (4 * p + 4))
                    for c in range(DC):
                        last = product(acc[:, c, :], [w[:, p, c * P:(c + 1) * P] for w in w_o],
                                       [a[:, :] for a in oT], p == 0, p == PAIRS - 1)
                    if p == PAIRS - 1:
                        last.then_inc(attn_done, 1)

                def turn_back(src, done):
                    for t in range(NT):
                        bank = (bank_o, bank_d)[t // 2]
                        for c in range(DC):
                            at = (t % 2) * D + c * P
                            last = pe.transpose(bank[:, at:at + P], src[:, c, t * P:(t + 1) * P], ident[:, :])
                    last.then_inc(done, 1)

                for p in range(PAIRS):
                    scores(p, 0)
                    scores(p, 1)
                    if p >= 2:
                        project_out(p - 2)
                    scores(p, 2)
                    if p + 1 < PAIRS:
                        project_qk(slot_for("qk", p + 1, 0), p + 1)
                    else:
                        slot = slot_for("turn1", 0, 0)
                        pe.wait_ge(xn_ready, i * 2 + 2)
                        turn_tokens(slot, x_next)
                    if p >= 1:
                        values(p - 1)
                    if p == PAIRS // 2:
                        for part in range(2):
                            project_v(slot_for("v", 1, part), 1, part)
                    if p >= 1:
                        denominators(p - 1)
                last_pair = PAIRS - 1
                project_out(last_pair - 1)
                slot = slot_for("qk", 0, 0)
                n = RING.index(("turn1", 0, 0))
                pe.wait_ge(dve_emptied, dves(emptied(n)[1]))
                project_qk(slot, 0)
                values(last_pair)
                project_v(slot_for("v", 0, 0), 0, 0)
                denominators(last_pair)
                project_v(slot_for("v", 0, 1), 0, 1)
                project_out(last_pair)
                pe.wait_ge(attn_copied, i * 2 + 2)
                turn_back(attnT, turned_attn)

                slot = slot_for("turn2", 0, 0)
                pe.wait_ge(xn_ready, i * 2 + 3)
                turn_tokens(slot, x_next)
                slot = slot_for("gate", 0, 0)
                n = RING.index(("turn2", 0, 0))
                pe.wait_ge(dve_emptied, dves(emptied(n)[1]))
                for t in range(NT):
                    for c in range(DC):
                        last = product(slot[:, 0, t * E:(t + 1) * E], [a[:, c, t * P:(t + 1) * P] for a in x2T],
                                       [w[:, c, :] for w in w_g], c == 0, c == DC - 1)
                last.then_inc(ring_full, 1)

                def hidden(e):
                    slot = slot_for("hidden", e, 0)
                    for f in range(FC):
                        for c in range(DC):
                            last = product(slot[:, f, :], [w[:, e, c, f * P:(f + 1) * P] for w in w_1],
                                           [a[:, c, :] for a in x2T], c == 0, c == DC - 1)
                    last.then_inc(ring_full, 1)

                def spread_weight(e):
                    bank = bank_o if e % 2 else bank_d
                    if e >= 3:
                        pe.wait_ge(h_steps, i * 26 + 3 * (e - 2))
                    pe.matmul(bank[:, :], pick[:, e - 1, :], combineT[:, :], start=True,
                              stop=True).then_inc(spread, 1)

                def expert_out(e):
                    pe.wait_ge(h_steps, i * 26 + (3 * e + 2))
                    for c in range(DC):
                        for f in range(FC):
                            last = product(acc[:, c, :], [w[:, e, f, c * P:(c + 1) * P] for w in w_2],
                                           [a[:, f, :] for a in hT[e % 2]], e == 0 and f == 0,
                                           e == NE - 1 and f == FC - 1)
                        if e == NE - 1:
                            last.then_inc(acc_done, 1)
                    if e < NE - 1:
                        last.then_inc(y_done, 1)

                hidden(0)
                hidden(1)
                pe.wait_ge(gate_steps, i * 12 + (2 + 12))
                for t in range(NT):
                    last = pe.transpose(bank_d[0:2 * E, t * P:(t + 1) * P], combine2[:, t, :].bitcast(F32),
                                        ident[:, :])
                last.then_inc(turned_gate, 1)
                expert_out(0)
                pe.wait_ge(combine_ready, i + 1)
                spread_weight(1)
                for c in range(DC):
                    for w in b_2:
                        pe.matmul(acc[:, c, :], w[:, c * P:(c + 1) * P], combineT[:, :], start=False,
                                  stop=False)
                for e in range(1, NE):
                    if e + 1 < NE:
                        hidden(e + 1)
                        spread_weight(e + 1)
                    expert_out(e)
                pe.wait_ge(y_copied, i * 2 + 2)
                turn_back(yT, turned_y)
                assert turn[0] == len(RING)


_OUT = "out_dram"


def kernel(L0_attn_x, L0_attn_Wq, L0_attn_Wk, L0_attn_Wv, L0_attn_Wo, L0_ffn_gate_w, L0_ffn_gate_b,
           L0_ffn_sw1, L0_ffn_sb1, L0_ffn_sw2, L0_ffn_sb2, L0_ffn_w1, L0_ffn_b1, L0_ffn_w2, L0_ffn_b2):
    import numpy as np
    import concourse.bacc as bacc
    from concourse.bass_utils import run_bass_kernel_spmd

    def laid(a):
        return np.ascontiguousarray(a)

    b1 = np.concatenate([np.asarray(L0_ffn_sb1)[None], np.asarray(L0_ffn_b1)])
    arrays = {
        "x": laid(L0_attn_x),
        "wqT": laid(np.asarray(L0_attn_Wq).T),
        "wkT": laid(np.asarray(L0_attn_Wk).T),
        "wvT": laid(np.asarray(L0_attn_Wv).T),
        "woT": laid(np.asarray(L0_attn_Wo).T),
        "gate_w": laid(L0_ffn_gate_w),
        "gate_b_rows": laid(np.broadcast_to(np.asarray(L0_ffn_gate_b), (P, E))),
        "w1s": laid(L0_ffn_sw1),
        "w1": laid(L0_ffn_w1),
        "w2s": laid(L0_ffn_sw2),
        "w2": laid(L0_ffn_w2),
        "b1_cols": laid(b1.reshape(NE, FC, P).transpose(2, 0, 1)),
        "b2_twice": laid(np.concatenate([np.asarray(L0_ffn_b2)] * 2)),
        "sb2_cols": laid(np.asarray(L0_ffn_sb2).reshape(DC, P).T),
    }
    nc = bacc.Bacc("TRN2", target_bir_lowering=False, num_devices=1)
    args = [nc.dram_tensor(f"in_{k}", a.shape, mybir.dt.from_np(a.dtype), kind="ExternalInput").ap()
            for k, a in arrays.items()]
    out = nc.dram_tensor(_OUT, (NSEQ, N, D), F32, kind="ExternalOutput").ap()
    block_program(nc, *args, out)
    r = run_bass_kernel_spmd(nc, [{f"in_{k}": a for k, a in arrays.items()}], core_ids=[0])
    return r.results[0][_OUT]
```

```python
from contextlib import ExitStack

import concourse.bass as bass
from concourse import mybir

F32 = mybir.dt.float32
F32R = mybir.dt.float32r
I32 = mybir.dt.int32
ALU = mybir.AluOpType
ACT = mybir.ActivationFunctionType
AX = mybir.AxisListType

P = 128
D = 256
DC = D // P
NSEQ, N = 16, 512
NT = N // P
H, DH = 16, 64
PAIRS = H // 2
HD = H * DH
FF = 256
FC = FF // P
E = 8
NE = E + 1
SOFTCLAMP = 50.0
SCALE = DH ** -0.5
EPS = 1e-5
RSQRT_GUESS = float(0x5F3759DF)
NEWTON = 3
STAGES = 2
LN_STEPS = 4 + 3 * NEWTON

SCORE_UNITS = [[(0, 0)], [(1, 0), (3, N - P)], [(2, 0)]]
UNIT_COLS = [N, N, N // 2]


def ring_plan():
    units = []
    for p in range(PAIRS):
        units += [("scores", p, u) for u in range(3)]
        if p + 1 < PAIRS:
            units.append(("qk", p + 1, 0))
        else:
            units.append(("turn1", 0, 0))
    units += [("v", t, 0) for t in range(NT)]
    units += [("turn2", 0, 0), ("gate", 0, 0)]
    units += [("hidden", e, 0) for e in range(NE)]
    units += [("qk", 0, 0)]
    return units


RING = ring_plan()
EMPTIED_BY_ACT = ("scores", "v", "hidden")
ACT_FIRST, DVE_FIRST = NT, 2
RING_FIRST = ACT_FIRST + DVE_FIRST
ACT_TURN = sum(k[0] in EMPTIED_BY_ACT for k in RING)
DVE_TURN = len(RING) - ACT_TURN
assert len(RING) % 2 == 0 and RING_FIRST % 2 == 0


def emptied(n):
    by_act = sum(k[0] in EMPTIED_BY_ACT for k in RING[:n + 1])
    return by_act, n + 1 - by_act


def block_program(nc, x, wqT, wkT, wvT, woT, gate_w, gate_b_rows, w1s, w1, w2s, w2,
                  b1_cols, b2_twice, sb2_cols, out):
    with ExitStack() as ctx:
        def sb(name, shape, dt=F32, stack=ctx):
            return stack.enter_context(nc.sbuf_tensor(name, shape, dt))

        def ps(name, shape):
            return ctx.enter_context(nc.psum_tensor(name, shape, F32))

        def sem(name):
            return ctx.enter_context(nc.semaphore(name))

        w_qk = [sb(f"w_qk{s}", [P, 2, DC, HD], F32R) for s in ("h", "l")]
        w_v = [sb(f"w_v{s}", [P, DC, HD], F32R) for s in ("h", "l")]
        w_o = [sb(f"w_o{s}", [P, PAIRS, D], F32R) for s in ("h", "l")]
        w_1 = [sb(f"w_1{s}", [P, NE, DC, FF], F32R) for s in ("h", "l")]
        w_2 = [sb(f"w_2{s}", [P, NE, FC, D], F32R) for s in ("h", "l")]
        w_g = [sb(f"w_g{s}", [P, DC, E], F32R) for s in ("h", "l")]
        b_2 = [sb(f"b_2{s}", [2 * E, D], F32R) for s in ("h", "l")]
        pick = sb("pick", [2 * E, E, P], F32R)
        b1c = sb("b1c", [P, NE, FC])
        sb2c = sb("sb2c", [P, DC])
        gate_b = sb("gate_b", [P, E])
        ident = sb("ident", [P, P])
        ones = sb("ones", [P, DH])
        lower = sb("lower", [P, E, E])

        x_next = sb("x_next", [P, NT, D])
        x_res = sb("x_res", [P, NT, D])
        xnT = [sb(f"xnT{s}", [P, DC, N], F32R) for s in ("h", "l")]
        qkT = [sb(f"qkT{s}", [P, 2, N], F32R) for s in ("h", "l")]
        x2T = qkT
        v = sb("v", [P, NT, HD])
        stats = sb("stats", [P, NT, 6])
        mean_var = sb("mean_var", [P, NT, 2])
        var_eps = sb("var_eps", [P, NT, 1])
        minus_half = sb("minus_half", [P, NT, 1])
        rstd = sb("rstd", [P, NT, 1])
        newton = sb("newton", [P, NT, 1])
        logit = sb("logit", [P, NT, E])
        row1 = sb("row1", [P, NT, 1])
        prob8 = sb("prob8", [P, NT, E])
        combine = sb("combine", [P, NT, E])
        combine2 = sb("combine2", [P, NT, 2 * E], F32R)

        with ExitStack() as arena:
            prob0 = [sb(f"prob0{k}", [P, 2, N], F32, arena) for k in range(2)]
            prob1 = sb("prob1", [P, 2, N], F32, arena)
            prob2 = sb("prob2", [P, 2, N // 2], F32, arena)
            key_sum = sb("key_sum", [P, 2, N - P], F32, arena)
            norm = sb("norm", [P, N], F32, arena)
            oT = [sb(f"oT{s}", [P, N], F32R, arena) for s in ("h", "l")]
        with ExitStack() as arena:
            attnT = sb("attnT", [P, DC, N], F32, arena)
        with ExitStack() as arena:
            hT = [[sb(f"hT{k}{s}", [P, FC, N], F32R, arena) for s in ("h", "l")] for k in range(2)]
            gelu = sb("gelu", [P, FC, N], F32, arena)
            combineT = sb("combineT", [2 * E, N], F32R, arena)
        with ExitStack() as arena:
            sb("under_yT", [P, 4 * N], F32, arena)
            yT = sb("yT", [P, DC, N], F32, arena)
        with ExitStack() as arena:
            stage = [sb(f"stage{k}", [P, 2048], F32, arena) for k in range(STAGES)]
            small = sb("small", [P, DC * E], F32, arena)
            small2 = sb("small2", [2 * E, D], F32, arena)
            pick_f = sb("pick_f", [2 * E, E, P], F32, arena)
        with ExitStack() as arena:
            sb("under_compare", [P, 4 * N], F32, arena)
            greater = sb("greater", [P, NT, E, E], F32, arena)
            equal = sb("equal", [P, NT, E, E], F32, arena)

        def prob(p, u):
            return (prob0[p % 2], prob1, prob2)[u]

        ring = [ps(f"ring{k}", [P, 2, N]) for k in range(2)]
        acc = ps("acc", [P, 2, N])
        bank_o = ps("bank_o", [P, N])
        bank_d = ps("bank_d", [P, N])

        small_loaded = sem("small_loaded")
        stage_loaded = [sem(f"stage_loaded{k}") for k in range(STAGES)]
        hi_split = sem("hi_split")
        lo_split = sem("lo_split")
        const_ready = sem("const_ready")
        xnext_loaded = sem("xnext_loaded")
        xres_loaded = sem("xres_loaded")
        stored = sem("stored")
        ring_full = sem("ring_full")
        act_emptied = sem("act_emptied")
        dve_emptied = sem("dve_emptied")
        turn_hi = sem("turn_hi")
        exp_done = sem("exp_done")
        masked = sem("masked")
        sum_steps = sem("sum_steps")
        den_done = sem("den_done")
        o_steps = sem("o_steps")
        projected = sem("projected")
        attn_copied = sem("attn_copied")
        turned_attn = sem("turned_attn")
        x1_ready = sem("x1_ready")
        ln_steps = sem("ln_steps")
        xn_ready = sem("xn_ready")
        gate_steps = sem("gate_steps")
        gate_exp = sem("gate_exp")
        turned_gate = sem("turned_gate")
        combine_ready = sem("combine_ready")
        spread = sem("spread")
        h_steps = sem("h_steps")
        y_done = sem("y_done")
        acc_done = sem("acc_done")
        y_copied = sem("y_copied")
        turned_y = sem("turned_y")
        out_ready = sem("out_ready")

        pieces = [
            ([(wvT.rearrange("(c p) f -> p c f", p=P), 0, 2048)], [w[:, :] for w in w_v], (DC, HD)),
            ([(wqT.rearrange("(c p) f -> p c f", p=P), 0, 2048)], [w[:, 0] for w in w_qk], (DC, HD)),
            ([(wkT.rearrange("(c p) f -> p c f", p=P), 0, 2048)], [w[:, 1] for w in w_qk], (DC, HD)),
            ([(woT.rearrange("(k p) d -> p k d", p=P), 0, 2048)], [w[:, :] for w in w_o], (PAIRS, D)),
        ]
        for shared, routed, dst in ((w1s, w1, w_1), (w2s, w2, w_2)):
            one = DC * FF
            pieces.append((
                [(shared.rearrange("(c p) f -> p c f", p=P), 0, one),
                 (routed[0:2].rearrange("e (c p) f -> p (e c) f", p=P), one, 3 * one)],
                [w[:, 0:3].rearrange("p e c f -> p (e c) f") for w in dst], (3 * DC, FF)))
            for e0 in (2, 5):
                pieces.append((
                    [(routed[e0:e0 + 3].rearrange("e (c p) f -> p (e c) f", p=P), 0, 3 * one)],
                    [w[:, e0 + 1:e0 + 4].rearrange("p e c f -> p (e c) f") for w in dst], (3 * DC, FF)))
        NPIECES = len(pieces)
        NPARTS = [0] * STAGES
        piece_loaded = []
        for k, (srcs, _, _) in enumerate(pieces):
            NPARTS[k % STAGES] += len(srcs)
            piece_loaded.append(16 * NPARTS[k % STAGES])

        def staged(k):
            (a, b) = pieces[k][2]
            return stage[k % STAGES][:, 0:a * b].rearrange("p (a b) -> p a b", a=a)

        x_tiles = x.rearrange("s (t p) d -> s p t d", p=P)
        out_tiles = out.rearrange("s (t p) d -> s p t d", p=P)
        

        block = ctx.enter_context(nc.Block())

        @block.sync
        def _(sp):
            sp.dma_start(x_next[:, :, :], x_tiles[0]).then_inc(xnext_loaded, 16)
            for k, (srcs, _, _) in enumerate(pieces):
                if k == 3:
                    sp.dma_start(small[:, :], gate_w.rearrange("(c p) e -> p c e", p=P)).then_inc(small_loaded, 16)
                    sp.dma_start(small2[:, :], b2_twice).then_inc(small_loaded, 16)
                    sp.dma_start(b1c[:, :, :], b1_cols).then_inc(small_loaded, 16)
                    sp.dma_start(sb2c[:, :], sb2_cols).then_inc(small_loaded, 16)
                    sp.dma_start(gate_b[:, :], gate_b_rows).then_inc(small_loaded, 16)
                if k >= STAGES:
                    sp.wait_ge(lo_split, k - STAGES + 1)
                for src, a, b in srcs:
                    dst = stage[k % STAGES][:, a:b].rearrange("p (a b) -> p a b", b=src.shape[2])
                    sp.dma_start(dst, src).then_inc(stage_loaded[k % STAGES], 16)
            sp.wait_ge(ring_full, 1)
            with sp.Fori(0, NSEQ) as i:
                sp.dma_start(x_next[:, :, :], x_tiles[(i + 1) % NSEQ]).then_inc(xnext_loaded, 16)
                sp.wait_ge(xnext_loaded, 16)
                sp.wait_ge(out_ready, i + 1)
                sp.dma_start(x_res[:, :, :], x_tiles[i]).then_inc(xres_loaded, 16)
                sp.wait_ge(out_ready, i + 2)
                sp.dma_start(out_tiles[i], x_next[:, :, :]).then_inc(stored, 16)
                stores = sp.to_reg(i * 16 + 16)
                sp.wait_ge(xnext_loaded, 16)
                sp.wait_ge(stored, stores)

        @block.gpsimd
        def _(pool):
            nc.gpsimd.memset(ident[:, :], 0.0)
            nc.gpsimd.memset(ones[:, :], 1.0)
            nc.gpsimd.memset(lower[:, :, :], 1.0)
            nc.gpsimd.memset(pick_f[:, :, :], 0.0).then_inc(const_ready, 1)
            pool.wait_ge(const_ready, 1)
            nc.gpsimd.affine_select(out=ident[:, :], in_=ident[:, :], compare_op=ALU.not_equal, fill=1.0,
                                    base=0, pattern=[[-1, P]], channel_multiplier=1)
            nc.gpsimd.affine_select(out=lower[:, :, :], in_=lower[:, :, :], compare_op=ALU.is_gt, fill=0.0,
                                    base=0, pattern=[[1, E], [-1, E]], channel_multiplier=0)
            nc.gpsimd.affine_select(out=pick_f[:, :, :], in_=pick_f[:, :, :], compare_op=ALU.not_equal,
                                    fill=1.0, base=0, pattern=[[-1, E], [0, P]],
                                    channel_multiplier=1).then_inc(const_ready, 1)
            pool.wait_ge(const_ready, 2)
            nc.gpsimd.affine_select(out=pick_f[:, :, :], in_=pick_f[:, :, :], compare_op=ALU.not_equal,
                                    fill=1.0, base=-E, pattern=[[-1, E], [0, P]],
                                    channel_multiplier=1).then_inc(const_ready, 1)

            with pool.Fori(0, NSEQ) as i:
                for p in range(PAIRS):
                    for u in range(3):
                        exps = pool.to_reg(i * 24 + (3 * p + u + 1))
                        pool.wait_ge(const_ready, 3)
                        pool.wait_ge(exp_done, exps)
                        for _, at in SCORE_UNITS[u]:
                            diag = prob(p, u)[:, :, at:at + P]
                            last = nc.gpsimd.affine_select(out=diag, in_=diag, compare_op=ALU.is_ge, fill=0.0,
                                                           base=0, pattern=[[0, 2], [1, P]],
                                                           channel_multiplier=-1)
                        last.then_inc(masked, 1)
                    t0, t13, t2 = prob(p, 0), prob(p, 1), prob(p, 2)
                    pool.wait_ge(masked, i * 24 + 3 * p + 3)
                    if p >= 1:
                        pool.wait_ge(den_done, i * 8 + p)
                    nc.gpsimd.tensor_tensor(key_sum[:, :, :], t0[:, :, P:N], t13[:, :, 0:N - P],
                                            ALU.add).then_inc(sum_steps, 1)
                    pool.wait_ge(sum_steps, i * 24 + 3 * p + 1)
                    nc.gpsimd.tensor_tensor(key_sum[:, :, P:], key_sum[:, :, P:], t2[:, :, :],
                                            ALU.add).then_inc(sum_steps, 1)
                    pool.wait_ge(sum_steps, i * 24 + 3 * p + 2)
                    nc.gpsimd.tensor_tensor(key_sum[:, :, 2 * P:], key_sum[:, :, 2 * P:], t13[:, :, N - P:],
                                            ALU.add).then_inc(sum_steps, 1)

        @block.scalar
        def _(act):
            def split_hi(k):
                act.wait_ge(stage_loaded[k % STAGES], piece_loaded[k])
                nc.scalar.copy(pieces[k][1][0], staged(k)).then_inc(hi_split, 1)

            for k in range(3):
                split_hi(k)

            def copy_v(slot, t, full):
                act.wait_ge(ring_full, full)
                nc.scalar.copy(v[:, t, :], slot[:, :, :].rearrange("p a n -> p (a n)")).then_inc(act_emptied, 1)

            for k in range(3, NPIECES):
                split_hi(k)
            for t in range(NT):
                copy_v(ring[(t + 1) % 2], t, t + 2)
            act.wait_ge(lo_split, NPIECES)
            with act.Fori(0, NSEQ) as i:
                def full(n):
                    return i * len(RING) + (RING_FIRST + n + 1)

                def exponentiate(n):
                    _, p, u = RING[n]
                    cols = prob(p, u)[:, :, :]
                    act.wait_ge(act_emptied, i * ACT_TURN + (ACT_FIRST + emptied(n)[0]))
                    nc.scalar.activation(cols, cols, ACT.Exp, scale=SOFTCLAMP).then_inc(exp_done, 1)

                waiting = None
                for n, (kind, a, b) in enumerate(RING):
                    slot = ring[n % 2]
                    if kind == "scores":
                        p, u = a, b
                        act.wait_ge(ring_full, full(n))
                        nc.scalar.activation(prob(p, u)[:, :, :], slot[:, :, 0:UNIT_COLS[u]],
                                             ACT.Tanh, scale=SCALE / SOFTCLAMP).then_inc(act_emptied, 1)
                        if waiting is not None:
                            exponentiate(waiting)
                        waiting = n
                    elif waiting is not None:
                        exponentiate(waiting)
                        waiting = None
                    if kind == "v":
                        copy_v(slot, a, full(n))
                        if a == 1:
                            act.wait_ge(projected, i * PAIRS + PAIRS)
                            nc.scalar.copy(attnT[:, 0, :], acc[:, 0, :]).then_inc(attn_copied, 1)
                        if a == NT - 1:
                            act.wait_ge(gate_steps, i * 12 + 4)
                            nc.scalar.activation(logit[:, :, :], logit[:, :, :], ACT.Exp).then_inc(gate_exp, 1)
                    if kind == "hidden":
                        e = a
                        act.wait_ge(ring_full, full(n))
                        if e >= 1:
                            act.wait_ge(h_steps, i * 26 + (3 * e - 1))
                        for c in range(FC):
                            last = nc.scalar.activation(gelu[:, c, :], slot[:, c, :], ACT.Gelu,
                                                        bias=b1c[:, e, c:c + 1])
                        last.then_inc(act_emptied, 1)
                act.wait_ge(acc_done, i * 2 + 1)
                nc.scalar.activation(yT[:, 0, :], acc[:, 0, :], ACT.Identity,
                                     bias=sb2c[:, 0:1]).then_inc(y_copied, 1)

        @block.vector
        def _(dve):
            def split_lo(k):
                dve.wait_ge(hi_split, k + 1)
                nc.vector.tensor_tensor(pieces[k][1][1], staged(k), pieces[k][1][0].bitcast(F32),
                                        ALU.subtract).then_inc(lo_split, 1)

            def layernorm_stats(src, steps):
                for t in range(NT):
                    last = nc.vector.bn_stats(stats[:, t, :], src[:, t, :])
                last.then_inc(ln_steps, 1)
                stats_done = dve.to_reg(steps + 1)
                dve.wait_ge(xnext_loaded, 16)
                dve.wait_ge(ln_steps, stats_done)
                for t in range(NT):
                    last = nc.vector.bn_aggr(mean_var[:, t, :], stats[:, t, :])
                last.then_inc(ln_steps, 1)
                dve.wait_ge(ln_steps, steps + 2)
                nc.vector.tensor_scalar(var_eps[:, :, :], mean_var[:, :, 1:2], EPS, None, ALU.add)
                nc.vector.tensor_scalar(minus_half[:, :, :], mean_var[:, :, 1:2], EPS, -0.5, ALU.add,
                                        ALU.mult).then_inc(ln_steps, 1)
                dve.wait_ge(ln_steps, steps + 3)
                nc.vector.tensor_scalar(rstd[:, :, :].bitcast(I32), var_eps[:, :, :].bitcast(I32), -0.5,
                                        RSQRT_GUESS, ALU.mult, ALU.add).then_inc(ln_steps, 1)
                for k in range(NEWTON):
                    dve.wait_ge(ln_steps, steps + (4 + 3 * k))
                    nc.vector.tensor_tensor(newton[:, :, :], rstd[:, :, :], rstd[:, :, :],
                                            ALU.mult).then_inc(ln_steps, 1)
                    dve.wait_ge(ln_steps, steps + (5 + 3 * k))
                    nc.vector.tensor_tensor(newton[:, :, :], newton[:, :, :], minus_half[:, :, :],
                                            ALU.mult).then_inc(ln_steps, 1)
                    dve.wait_ge(ln_steps, steps + (6 + 3 * k))
                    nc.vector.scalar_tensor_tensor(rstd[:, :, :], newton[:, :, :], 1.5, rstd[:, :, :],
                                                   ALU.add, ALU.mult).then_inc(ln_steps, 1)

            def layernorm_apply(src, steps):
                dve.wait_ge(ln_steps, steps + LN_STEPS)
                for t in range(NT):
                    last = nc.vector.tensor_scalar(x_next[:, t, :], src[:, t, :], mean_var[:, t, 0:1],
                                                   rstd[:, t, :], ALU.subtract, ALU.mult)
                last.then_inc(xn_ready, 1)

            def empty_split(dst, slot, full, his):
                dve.wait_ge(ring_full, full)
                nc.vector.tensor_copy(dst[0][:, :, :], slot[:, :, :]).then_inc(turn_hi, 1)
                dve.wait_ge(turn_hi, his)
                nc.vector.tensor_tensor(dst[1][:, :, :], slot[:, :, :], dst[0][:, :, :].bitcast(F32),
                                        ALU.subtract).then_inc(dve_emptied, 1)

            dve.wait_ge(xnext_loaded, 16)
            layernorm_stats(x_next, 0)
            layernorm_apply(x_next, 0)
            split_lo(0)
            dve.wait_ge(const_ready, 3)
            nc.vector.tensor_copy(pick[:, :, :], pick_f[:, :, :]).then_inc(out_ready, 1)
            empty_split(xnT, ring[0], 1, 1)
            split_lo(1)
            split_lo(2)
            dve.wait_ge(small_loaded, 16 * 5)
            g3 = small[:, :].rearrange("p (c e) -> p c e", c=DC)
            nc.vector.tensor_copy(w_g[0][:, :, :], g3)
            nc.vector.tensor_copy(b_2[0][:, :], small2[:, :]).then_inc(gate_steps, 1)
            dve.wait_ge(gate_steps, 1)
            nc.vector.tensor_tensor(w_g[1][:, :, :], g3, w_g[0][:, :, :].bitcast(F32), ALU.subtract)
            nc.vector.tensor_tensor(b_2[1][:, :], small2[:, :], b_2[0][:, :].bitcast(F32),
                                    ALU.subtract).then_inc(gate_steps, 1)
            dve.wait_ge(gate_steps, 2)
            for k in range(3, NPIECES):
                split_lo(k)
            empty_split(qkT, ring[1], RING_FIRST, 2)

            with dve.Fori(0, NSEQ) as i:
                def full(n):
                    return i * len(RING) + (RING_FIRST + n + 1)

                def his(n):
                    return i * (DVE_TURN - 1) + (DVE_FIRST + emptied(n)[1] - (n > RING.index(("gate", 0, 0))))

                def normalise(p):
                    dve.wait_ge(den_done, i * 8 + (p + 1))
                    nc.vector.reciprocal(norm[:, :], bank_d[:, :]).then_inc(o_steps, 1)
                    dve.wait_ge(o_steps, i * 32 + (4 * p + 1))
                    nc.vector.tensor_tensor(norm[:, :], bank_o[:, :], norm[:, :], ALU.mult).then_inc(o_steps, 1)
                    dve.wait_ge(o_steps, i * 32 + (4 * p + 2))
                    if p >= 1:
                        dve.wait_ge(projected, i * PAIRS + p)
                    nc.vector.tensor_copy(oT[0][:, :], norm[:, :]).then_inc(o_steps, 1)
                    dve.wait_ge(o_steps, i * 32 + (4 * p + 3))
                    nc.vector.tensor_tensor(oT[1][:, :], norm[:, :], oT[0][:, :].bitcast(F32),
                                            ALU.subtract).then_inc(o_steps, 1)

                for p in range(PAIRS):
                    if p == 6:
                        layernorm_apply(x_next, i * (2 * LN_STEPS) + LN_STEPS)
                    if p >= 1:
                        normalise(p - 1)
                    if p + 1 < PAIRS:
                        n = RING.index(("qk", p + 1, 0))
                        empty_split(qkT, ring[n % 2], full(n), his(n))
                    else:
                        n = RING.index(("turn1", 0, 0))
                        empty_split(xnT, ring[n % 2], full(n), his(n))
                    if p == 5:
                        dve.wait_ge(xnext_loaded, i * 16 + 32)
                        layernorm_stats(x_next, i * (2 * LN_STEPS) + LN_STEPS)
                normalise(PAIRS - 1)

                dve.wait_ge(projected, i * PAIRS + PAIRS)
                nc.vector.tensor_copy(attnT[:, 1, :], acc[:, 1, :]).then_inc(attn_copied, 1)
                dve.wait_ge(turned_attn, i + 1)
                dve.wait_ge(xres_loaded, i * 16 + 16)
                for k, bank in enumerate((bank_o, bank_d)):
                    half = x_res[:, 2 * k:2 * k + 2, :].rearrange("p t d -> p (t d)")
                    last = nc.vector.tensor_tensor(half, half, bank[:, :], ALU.add)
                last.then_inc(x1_ready, 1)
                dve.wait_ge(x1_ready, i + 1)
                layernorm_stats(x_res, i * (2 * LN_STEPS) + 2 * LN_STEPS)
                layernorm_apply(x_res, i * (2 * LN_STEPS) + 2 * LN_STEPS)
                n = RING.index(("turn2", 0, 0))
                empty_split(x2T, ring[n % 2], full(n), his(n))

                n = RING.index(("gate", 0, 0))
                gates = ring[n % 2][:, 0, 0:NT * E].rearrange("p (t e) -> p t e", t=NT)
                step = [0]

                def then(ins):
                    step[0] += 1
                    ins.then_inc(gate_steps, 1)
                    dve.wait_ge(gate_steps, i * 12 + (2 + step[0]))

                dve.wait_ge(ring_full, full(n))
                nc.vector.tensor_tensor(logit[:, :, :], gates, gate_b[:, None, :].to_broadcast([P, NT, E]),
                                        ALU.add).then_inc(dve_emptied, 1)
                dve.wait_ge(dve_emptied, i * DVE_TURN + (DVE_FIRST + emptied(n)[1]))
                then(nc.vector.tensor_reduce(row1[:, :, :], logit[:, :, :], AX.X, ALU.max))
                then(nc.vector.tensor_tensor(logit[:, :, :], logit[:, :, :],
                                             row1[:, :, :].to_broadcast([P, NT, E]), ALU.subtract))
                dve.wait_ge(gate_exp, i + 1)
                then(nc.vector.tensor_reduce(row1[:, :, :], logit[:, :, :], AX.X, ALU.add))
                then(nc.vector.reciprocal(row1[:, :, :], row1[:, :, :]))
                then(nc.vector.tensor_tensor(prob8[:, :, :], logit[:, :, :],
                                             row1[:, :, :].to_broadcast([P, NT, E]), ALU.mult))
                shape = [P, NT, E, E]
                other = prob8[:, :, None, :].to_broadcast(shape)
                own = prob8[:, :, :, None].to_broadcast(shape)
                nc.vector.tensor_tensor(greater[:, :, :, :], other, own, ALU.is_gt)
                then(nc.vector.tensor_tensor(equal[:, :, :, :], other, own, ALU.is_equal))
                then(nc.vector.tensor_tensor(equal[:, :, :, :], equal[:, :, :, :],
                                             lower[:, None, :, :].to_broadcast(shape), ALU.mult))
                then(nc.vector.tensor_tensor(greater[:, :, :, :], greater[:, :, :, :], equal[:, :, :, :],
                                             ALU.add))
                then(nc.vector.tensor_reduce(combine[:, :, :], greater[:, :, :, :], AX.X, ALU.add))
                then(nc.vector.scalar_tensor_tensor(combine[:, :, :], combine[:, :, :], 2.0, prob8[:, :, :],
                                                    ALU.is_lt, ALU.mult))
                then(nc.vector.tensor_copy(combine2[:, :, 0:E], combine[:, :, :]))
                then(nc.vector.tensor_tensor(combine2[:, :, E:], combine[:, :, :],
                                             combine2[:, :, 0:E].bitcast(F32), ALU.subtract))
                assert step[0] == 12
                dve.wait_ge(turned_gate, i + 1)
                nc.vector.tensor_copy(combineT[:, :], bank_d[0:2 * E, :]).then_inc(combine_ready, 1)

                for e in range(NE):
                    n = RING.index(("hidden", e, 0))
                    dve.wait_ge(act_emptied, i * ACT_TURN + (ACT_FIRST + emptied(n)[0]))
                    if e >= 1:
                        bank = bank_o if e % 2 else bank_d
                        dve.wait_ge(spread, i * 8 + e)
                        nc.vector.tensor_tensor(gelu[:, :, :], gelu[:, :, :],
                                                bank[:, None, :].to_broadcast([P, FC, N]),
                                                ALU.mult).then_inc(h_steps, 1)
                        dve.wait_ge(h_steps, i * 26 + 3 * e)
                    if e >= 2:
                        dve.wait_ge(y_done, i * 8 + (e - 1))
                    hh, hl = hT[e % 2]
                    nc.vector.tensor_copy(hh[:, :, :], gelu[:, :, :]).then_inc(h_steps, 1)
                    dve.wait_ge(h_steps, i * 26 + (3 * e + 1))
                    nc.vector.tensor_tensor(hl[:, :, :], gelu[:, :, :], hh[:, :, :].bitcast(F32),
                                            ALU.subtract).then_inc(h_steps, 1)

                n = RING.index(("qk", 0, 0))
                empty_split(qkT, ring[n % 2], full(n), his(n))
                dve.wait_ge(acc_done, i * 2 + 2)
                nc.vector.tensor_scalar(yT[:, 1, :], acc[:, 1, :], sb2c[:, 1:2], None,
                                        ALU.add).then_inc(y_copied, 1)
                dve.wait_ge(turned_y, i + 1)
                for k, bank in enumerate((bank_o, bank_d)):
                    half = slice(2 * k, 2 * k + 2)
                    last = nc.vector.tensor_tensor(x_next[:, half, :].rearrange("p t d -> p (t d)"),
                                                   x_res[:, half, :].rearrange("p t d -> p (t d)"),
                                                   bank[:, :], ALU.add)
                last.then_inc(out_ready, 1)

        @block.tensor
        def _(pe):
            def product(dst, w, m, start, stop):
                pe.matmul(dst, w[0], m[0], start=start, stop=False)
                pe.matmul(dst, w[0], m[1], start=False, stop=False)
                return pe.matmul(dst, w[1], m[0], start=False, stop=stop)

            def turn_tokens(slot, src):
                for c in range(DC):
                    for t in range(NT):
                        last = pe.transpose(slot[:, c, t * P:(t + 1) * P], src[:, t, c * P:(c + 1) * P],
                                            ident[:, :])
                last.then_inc(ring_full, 1)

            def project_qk(slot, p):
                for m in range(2):
                    for c in range(DC):
                        last = product(slot[:, m, :], [w[:, m, c, p * P:(p + 1) * P] for w in w_qk],
                                       [a[:, c, :] for a in xnT], c == 0, c == DC - 1)
                last.then_inc(ring_full, 1)

            def project_v(slot, t):
                for k in range(2):
                    for c in range(DC):
                        last = product(slot[:, k, :], [a[:, c, t * P:(t + 1) * P] for a in xnT],
                                       [w[:, c, k * N:(k + 1) * N] for w in w_v], c == 0, c == DC - 1)
                last.then_inc(ring_full, 1)

            pe.wait_ge(const_ready, 3)
            pe.wait_ge(xn_ready, 1)
            turn_tokens(ring[0], x_next)
            pe.wait_ge(lo_split, 1)
            pe.wait_ge(dve_emptied, 1)
            for t in range(NT):
                if t >= 2:
                    pe.wait_ge(act_emptied, t - 1)
                project_v(ring[(t + 1) % 2], t)
            pe.wait_ge(lo_split, 3)
            pe.wait_ge(act_emptied, NT - 1)
            project_qk(ring[1], 0)
            pe.wait_ge(lo_split, NPIECES)
            pe.wait_ge(gate_steps, 2)

            with pe.Fori(0, NSEQ) as i:
                def acts(k):
                    return i * ACT_TURN + (ACT_FIRST + k)

                def dves(k):
                    return i * DVE_TURN + (DVE_FIRST + k)

                turn = [0]

                def slot_for(*unit):
                    n = turn[0]
                    assert RING[n] == unit
                    turn[0] += 1
                    if n == 0:
                        pe.wait_ge(act_emptied, acts(0))
                    elif n == 1:
                        pe.wait_ge(dve_emptied, dves(0))
                    elif RING[n - 2][0] in EMPTIED_BY_ACT:
                        pe.wait_ge(act_emptied, acts(emptied(n - 2)[0]))
                    else:
                        pe.wait_ge(dve_emptied, dves(emptied(n - 2)[1]))
                    return ring[n % 2]

                def scores(p, u):
                    slot = slot_for("scores", p, u)
                    if u == 0:
                        n = RING.index(("qk", p, 0)) if p else -1
                        pe.wait_ge(dve_emptied, dves(emptied(n)[1] if p else 0))
                    for j, at in SCORE_UNITS[u]:
                        q = slice(j * P, N)
                        for n, (a, b) in enumerate(((0, 0), (0, 1), (1, 0))):
                            for h in range(2):
                                r = slice(h * DH, (h + 1) * DH)
                                last = pe.matmul(slot[:, h, at:at + N - j * P],
                                                 qkT[a][r, 1, j * P:(j + 1) * P], qkT[b][r, 0, q],
                                                 start=(n == 0), stop=(n == 2))
                    last.then_inc(ring_full, 1)

                def values(p):
                    if p == 0:
                        pe.wait_ge(out_ready, i + 1)
                    else:
                        pe.wait_ge(o_steps, i * 32 + (4 * p - 2))
                    units = [(u, j, at) for u in range(3) for j, at in SCORE_UNITS[u]]
                    for k, (u, j, at) in enumerate(units):
                        pe.wait_ge(masked, i * 24 + (3 * p + u + 1))
                        for h in range(2):
                            f = p * P + h * DH
                            pe.matmul(bank_o[h * DH:(h + 1) * DH, j * P:N], v[:, j, f:f + DH],
                                      prob(p, u)[:, h, at:at + N - j * P],
                                      start=(k == 0), stop=(k == len(units) - 1))

                def denominators(p):
                    pe.wait_ge(sum_steps, i * 24 + (3 * p + 3))
                    for h in range(2):
                        pe.matmul(bank_d[h * DH:(h + 1) * DH, 0:P], ones[:, :],
                                  prob(p, 0)[:, h, 0:P], start=True, stop=True)
                    for h in range(2):
                        last = pe.matmul(bank_d[h * DH:(h + 1) * DH, P:N], ones[:, :], key_sum[:, h, :],
                                         start=True, stop=True)
                    last.then_inc(den_done, 1)

                def project_out(p):
                    pe.wait_ge(o_steps, i * 32 + (4 * p + 4))
                    for c in range(DC):
                        last = product(acc[:, c, :], [w[:, p, c * P:(c + 1) * P] for w in w_o],
                                       [a[:, :] for a in oT], p == 0, p == PAIRS - 1)
                    last.then_inc(projected, 1)

                def turn_back(src, done):
                    for t in range(NT):
                        bank = (bank_o, bank_d)[t // 2]
                        for c in range(DC):
                            at = (t % 2) * D + c * P
                            last = pe.transpose(bank[:, at:at + P], src[:, c, t * P:(t + 1) * P], ident[:, :])
                    last.then_inc(done, 1)

                for p in range(PAIRS):
                    scores(p, 0)
                    if p >= 1:
                        denominators(p - 1)
                    scores(p, 1)
                    if 2 <= p < PAIRS - 1:
                        project_out(p - 2)
                    scores(p, 2)
                    if p + 1 < PAIRS:
                        project_qk(slot_for("qk", p + 1, 0), p + 1)
                    else:
                        slot = slot_for("turn1", 0, 0)
                        pe.wait_ge(xn_ready, i * 2 + 2)
                        turn_tokens(slot, x_next)
                        project_out(p - 2)
                    values(p)
                last_pair = PAIRS - 1
                slot = slot_for("v", 0, 0)
                n = RING.index(("turn1", 0, 0))
                pe.wait_ge(dve_emptied, dves(emptied(n)[1]))
                project_v(slot, 0)
                denominators(last_pair)
                project_out(last_pair - 1)
                project_v(slot_for("v", 1, 0), 1)
                project_out(last_pair)
                project_v(slot_for("v", 2, 0), 2)
                pe.wait_ge(attn_copied, i * 2 + 2)
                turn_back(attnT, turned_attn)
                project_v(slot_for("v", 3, 0), 3)

                slot = slot_for("turn2", 0, 0)
                pe.wait_ge(xn_ready, i * 2 + 3)
                turn_tokens(slot, x_next)
                slot = slot_for("gate", 0, 0)
                n = RING.index(("turn2", 0, 0))
                pe.wait_ge(dve_emptied, dves(emptied(n)[1]))
                for t in range(NT):
                    for c in range(DC):
                        last = product(slot[:, 0, t * E:(t + 1) * E], [a[:, c, t * P:(t + 1) * P] for a in x2T],
                                       [w[:, c, :] for w in w_g], c == 0, c == DC - 1)
                last.then_inc(ring_full, 1)

                def hidden(e):
                    slot = slot_for("hidden", e, 0)
                    for f in range(FC):
                        for c in range(DC):
                            last = product(slot[:, f, :], [w[:, e, c, f * P:(f + 1) * P] for w in w_1],
                                           [a[:, c, :] for a in x2T], c == 0, c == DC - 1)
                    last.then_inc(ring_full, 1)

                def spread_weight(e):
                    bank = bank_o if e % 2 else bank_d
                    if e >= 3:
                        pe.wait_ge(h_steps, i * 26 + 3 * (e - 2))
                    pe.matmul(bank[:, :], pick[:, e - 1, :], combineT[:, :], start=True,
                              stop=True).then_inc(spread, 1)

                def expert_out(e):
                    pe.wait_ge(h_steps, i * 26 + (3 * e + 2))
                    for c in range(DC):
                        for f in range(FC):
                            last = product(acc[:, c, :], [w[:, e, f, c * P:(c + 1) * P] for w in w_2],
                                           [a[:, f, :] for a in hT[e % 2]], e == 0 and f == 0,
                                           e == NE - 1 and f == FC - 1)
                        if e == NE - 1:
                            last.then_inc(acc_done, 1)
                    if e < NE - 1:
                        last.then_inc(y_done, 1)

                hidden(0)
                hidden(1)
                pe.wait_ge(gate_steps, i * 12 + (2 + 12))
                for t in range(NT):
                    last = pe.transpose(bank_d[0:2 * E, t * P:(t + 1) * P], combine2[:, t, :].bitcast(F32),
                                        ident[:, :])
                last.then_inc(turned_gate, 1)
                hidden(2)
                pe.wait_ge(combine_ready, i + 1)
                spread_weight(1)
                expert_out(0)
                for c in range(DC):
                    for w in b_2:
                        pe.matmul(acc[:, c, :], w[:, c * P:(c + 1) * P], combineT[:, :], start=False,
                                  stop=False)
                for e in range(1, NE):
                    if e + 2 < NE:
                        hidden(e + 2)
                    if e + 1 < NE:
                        spread_weight(e + 1)
                    if e == NE - 1:
                        project_qk(slot_for("qk", 0, 0), 0)
                    expert_out(e)
                pe.wait_ge(y_copied, i * 2 + 2)
                turn_back(yT, turned_y)
                assert turn[0] == len(RING)


_OUT = "out_dram"


def kernel(L0_attn_x, L0_attn_Wq, L0_attn_Wk, L0_attn_Wv, L0_attn_Wo, L0_ffn_gate_w, L0_ffn_gate_b,
           L0_ffn_sw1, L0_ffn_sb1, L0_ffn_sw2, L0_ffn_sb2, L0_ffn_w1, L0_ffn_b1, L0_ffn_w2, L0_ffn_b2):
    import numpy as np
    import concourse.bacc as bacc
    from concourse.bass_utils import run_bass_kernel_spmd

    def laid(a):
        return np.ascontiguousarray(a)

    b1 = np.concatenate([np.asarray(L0_ffn_sb1)[None], np.asarray(L0_ffn_b1)])
    arrays = {
        "x": laid(L0_attn_x),
        "wqT": laid(np.asarray(L0_attn_Wq).T),
        "wkT": laid(np.asarray(L0_attn_Wk).T),
        "wvT": laid(np.asarray(L0_attn_Wv).T),
        "woT": laid(np.asarray(L0_attn_Wo).T),
        "gate_w": laid(L0_ffn_gate_w),
        "gate_b_rows": laid(np.broadcast_to(np.asarray(L0_ffn_gate_b), (P, E))),
        "w1s": laid(L0_ffn_sw1),
        "w1": laid(L0_ffn_w1),
        "w2s": laid(L0_ffn_sw2),
        "w2": laid(L0_ffn_w2),
        "b1_cols": laid(b1.reshape(NE, FC, P).transpose(2, 0, 1)),
        "b2_twice": laid(np.concatenate([np.asarray(L0_ffn_b2)] * 2)),
        "sb2_cols": laid(np.asarray(L0_ffn_sb2).reshape(DC, P).T),
    }
    nc = bacc.Bacc("TRN2", target_bir_lowering=False, num_devices=1)
    args = [nc.dram_tensor(f"in_{k}", a.shape, mybir.dt.from_np(a.dtype), kind="ExternalInput").ap()
            for k, a in arrays.items()]
    out = nc.dram_tensor(_OUT, (NSEQ, N, D), F32, kind="ExternalOutput").ap()
    block_program(nc, *args, out)
    r = run_bass_kernel_spmd(nc, [{f"in_{k}": a for k, a in arrays.items()}], core_ids=[0])
    return r.results[0][_OUT]
```

```python
from contextlib import ExitStack

import concourse.bass as bass
from concourse import mybir

F32 = mybir.dt.float32
F32R = mybir.dt.float32r
I32 = mybir.dt.int32
ALU = mybir.AluOpType
ACT = mybir.ActivationFunctionType
AX = mybir.AxisListType

P = 128
D = 256
DC = D // P
NSEQ, N = 16, 512
NT = N // P
H, DH = 16, 64
PAIRS = H // 2
HD = H * DH
FF = 256
FC = FF // P
E = 8
NE = E + 1
SOFTCLAMP = 50.0
SCALE = DH ** -0.5
EPS = 1e-5
RSQRT_GUESS = float(0x5F3759DF)
NEWTON = 3
LN_STEPS = 4 + 3 * NEWTON

SCORE_UNITS = [[(0, 0)], [(1, 0), (3, N - P)], [(2, 0)]]
UNIT_COLS = [N, N, N // 2]
SUMS = 3 * (PAIRS - 1) - 2


def ring_plan():
    units = [("scores", 0, 2), ("qk", 1, 0)]
    for p in range(1, PAIRS):
        if p + 1 < PAIRS:
            units += [("scores", p, 0), ("scores", p, 1), ("scores", p, 2), ("qk", p + 1, 0)]
        else:
            units += [("scores", p, 0), ("turn1", 0, 0), ("scores", p, 1), ("scores", p, 2)]
    units += [("v", 0, 0), ("attn", 0, 0)] + [("v", t, 0) for t in range(1, NT)]
    units += [("turn2", 0, 0)]
    units += [("hidden", e, 0) for e in range(NE)]
    units += [("qk", 0, 0), ("scores", 0, 0), ("scores", 0, 1)]
    return units


RING = ring_plan()
TURN2 = RING.index(("turn2", 0, 0))
ATTN = RING.index(("attn", 0, 0))
EMPTIED_BY_ACT = ("scores", "v", "hidden")
ACT_FIRST, DVE_FIRST = NT + 2, 2
RING_FIRST = ACT_FIRST + DVE_FIRST
ACT_TURN = sum(k[0] in EMPTIED_BY_ACT for k in RING)
DVE_TURN = len(RING) - ACT_TURN
assert len(RING) % 2 == 0


HI_FIRST = 3
HI_TURN = 3 * PAIRS - 1


def qk_his(p):
    return HI_FIRST + 3 * (p or PAIRS) - 1


def slot_index(n):
    return (RING_FIRST + n) % 2


def emptied(n):
    by_act = sum(k[0] in EMPTIED_BY_ACT for k in RING[:n + 1])
    return by_act, n + 1 - by_act


def block_program(nc, x, wqT, wkT, wvT, woT, gate_w, gate_b_rows, w1s, w1, w2s, w2,
                  b1_cols, b2_twice, sb2_cols, out):
    with ExitStack() as ctx:
        def sb(name, shape, dt=F32, stack=ctx):
            return stack.enter_context(nc.sbuf_tensor(name, shape, dt))

        def ps(name, shape):
            return ctx.enter_context(nc.psum_tensor(name, shape, F32))

        def sem(name):
            return ctx.enter_context(nc.semaphore(name))

        GATE = DC * E
        sizes = {"w_qk": 2 * DC * HD, "w_v": DC * HD, "w_o": PAIRS * D, "w_1": GATE + NE * DC * FF,
                 "w_2": NE * FC * D}
        split = {name: [sb(f"{name}h", [P, n], F32R)] for name, n in sizes.items()}
        with ExitStack() as loads:
            raw = {name: sb(f"{name}_raw", [P, n], F32, loads) for name, n in sizes.items()}
        for name, n in sizes.items():
            split[name].append(sb(f"{name}l", [P, n], F32R))
        w_qk = [w[:, :].rearrange("p (m c f) -> p m c f", m=2, c=DC) for w in split["w_qk"]]
        w_v = [w[:, :].rearrange("p (c f) -> p c f", c=DC) for w in split["w_v"]]
        w_o = [w[:, :].rearrange("p (k d) -> p k d", k=PAIRS) for w in split["w_o"]]
        w_g = [w[:, 0:GATE + P] for w in split["w_1"]]
        w_1 = [w[:, GATE:].rearrange("p (e c f) -> p e c f", e=NE, c=DC) for w in split["w_1"]]
        w_2 = [w[:, :].rearrange("p (e c d) -> p e c d", e=NE, c=FC) for w in split["w_2"]]
        b_2 = [sb(f"b_2{s}", [2 * E, D], F32R) for s in ("h", "l")]
        pick = sb("pick", [2 * E, E], F32R)
        b1c = sb("b1c", [P, NE, FC])
        sb2c = sb("sb2c", [P, DC])
        gate_b = sb("gate_b", [E, 1])
        ident = sb("ident", [P, P])
        ones = sb("ones", [P, DH])
        table_call = sb("table_call", [P, 1])
        lower = sb("lower", [P, E, E])

        x_next = sb("x_next", [P, NT, D])
        x_res = sb("x_res", [P, NT, D])
        xnT = [sb(f"xnT{s}", [P, DC, N], F32R) for s in ("h", "l")]
        with ExitStack() as arena:
            x2T = [sb(f"x2T{s}", [P, DC, N], F32R, arena) for s in ("h", "l")]
        kT = sb("kT", [P, 2, N], F32R)
        qT = sb("qT", [P, 2, N], F32R)
        q_lo = sb("q_lo", [P, N], F32R)
        head_rows = [slice(0, DH), slice(DH, P)]
        v = sb("v", [P, NT, HD])
        stats = sb("stats", [P, NT, 6])
        mean_var = sb("mean_var", [P, NT, 2])
        var_eps = sb("var_eps", [P, NT, 1])
        minus_half = sb("minus_half", [P, NT, 1])
        rstd = sb("rstd", [P, NT, 1])
        newton = sb("newton", [P, NT, 1])
        last_recip = sb("last_recip", [P, NT, 2])
        logit = sb("logit", [P, NT, E])
        row1 = sb("row1", [P, NT, 1])
        prob8 = sb("prob8", [P, NT, E])
        combine = sb("combine", [P, NT, E])
        combine2 = sb("combine2", [P, NT, 2 * E], F32R)

        with ExitStack() as arena:
            prob0 = [sb(f"prob0{k}", [P, 2, N], F32, arena) for k in range(2)]
            prob1 = sb("prob1", [P, 2, N], F32, arena)
            prob2 = sb("prob2", [P, 2, N // 2], F32, arena)
            key_sum = sb("key_sum", [P, 2, N - P], F32, arena)
            norm = sb("norm", [P, N], F32, arena)
            oT = [sb(f"oT{s}", [P, N], F32R, arena) for s in ("h", "l")]
        with ExitStack() as arena:
            last_oT = [sb(f"last_oT{s}", [P, N], F32R, arena) for s in ("h", "l")]
            attnT = sb("attnT", [P, DC, N], F32, arena)
        with ExitStack() as arena:
            hT = [[sb(f"hT{k}{s}", [P, FC, N], F32R, arena) for s in ("h", "l")] for k in range(2)]
            gelu = sb("gelu", [P, FC, N], F32, arena)
            combineT = sb("combineT", [2 * E, N], F32R, arena)
        with ExitStack() as arena:
            sb("under_gateT", [P, 5 * FC * N], F32, arena)
            gateT = sb("gateT", [E, N], F32, arena)
        with ExitStack() as arena:
            sb("under_yT", [P, 8 * N], F32, arena)
            yT = sb("yT", [P, DC, N], F32, arena)
        with ExitStack() as arena:
            small2 = sb("small2", [2 * E, D], F32, arena)
            pick_f = sb("pick_f", [2 * E, E], F32, arena)
        with ExitStack() as arena:
            sb("under_compare", [P, 4 * N], F32, arena)
            greater = sb("greater", [P, NT, E, E], F32, arena)
            equal = sb("equal", [P, NT, E, E], F32, arena)

        def prob(p, u):
            return (prob0[p % 2], prob1, prob2)[u]

        def x2_half(part, k):
            return (x2T[part][:, :, k * (N // 2):(k + 1) * (N // 2)],
                    ring[slot_index(TURN2)][:, k, :].rearrange("p (c n) -> p c n", c=DC))

        ring = [ps(f"ring{k}", [P, 2, N]) for k in range(2)]
        acc = ps("acc", [P, 2, N])
        bank_o = ps("bank_o", [P, N])
        bank_d = ps("bank_d", [P, N])

        small_loaded = sem("small_loaded")
        hi_split = sem("hi_split")
        lo_split = sem("lo_split")
        pool_hi = sem("pool_hi")
        pool_lo = sem("pool_lo")
        const_ready = sem("const_ready")
        xnext_loaded = sem("xnext_loaded")
        xres_loaded = sem("xres_loaded")
        stored = sem("stored")
        ring_full = sem("ring_full")
        act_emptied = sem("act_emptied")
        dve_emptied = sem("dve_emptied")
        qk_hi = sem("qk_hi")
        k1_hi = sem("k1_hi")
        k_lo = sem("k_lo")
        exp_done = sem("exp_done")
        masked = sem("masked")
        sum_steps = sem("sum_steps")
        den_done = sem("den_done")
        last_values = sem("last_values")
        o_steps = sem("o_steps")
        projected = sem("projected")
        out_copied = sem("out_copied")
        last_spread = sem("last_spread")
        attn_done = sem("attn_done")
        attn_copied = [sem(f"attn_copied{c}") for c in range(DC)]
        turned_attn = sem("turned_attn")
        turned2 = sem("turned2")
        first_sums = sem("first_sums")
        last_sums = sem("last_sums")
        xn_hi = sem("xn_hi")
        xn_half = sem("xn_half")
        x2_hi = sem("x2_hi")
        k_projected = sem("k_projected")
        turned_logits = sem("turned_logits")
        gated = sem("gated")
        gate_copied = sem("gate_copied")
        ln_steps = sem("ln_steps")
        xn_ready = sem("xn_ready")
        gate_steps = sem("gate_steps")
        gate_exp = sem("gate_exp")
        turned_gate = sem("turned_gate")
        combine_ready = sem("combine_ready")
        spread = sem("spread")
        h_steps = sem("h_steps")
        y_done = sem("y_done")
        acc_done = sem("acc_done")
        y_copied = [sem(f"y_copied{c}") for c in range(DC)]
        turned_y = sem("turned_y")
        out_ready = sem("out_ready")

        def rows(a):
            return a.rearrange("(c p) f -> p c f", p=P)

        def cols(name, a, b, src):
            return raw[name][:, a:b].rearrange("p (a b) -> p a b", b=src.shape[2]), src

        one = DC * FF
        loads = [
            cols("w_qk", DC * HD, 2 * DC * HD, rows(wkT)),
            cols("w_qk", 0, DC * HD, rows(wqT)),
            cols("w_v", 0, DC * HD, rows(wvT)),
            cols("w_o", 0, PAIRS * D, rows(woT)),
            cols("w_1", 0, GATE, rows(gate_w)),
            cols("w_1", GATE, GATE + one, rows(w1s)),
            cols("w_1", GATE + one, GATE + NE * one, w1.rearrange("e (c p) f -> p (e c) f", p=P)),
            cols("w_2", 0, one, rows(w2s)),
            cols("w_2", one, NE * one, w2.rearrange("e (c p) f -> p (e c) f", p=P)),
        ]
        loaded = [sem(f"loaded{k}") for k in range(len(loads))]
        half_1, half_2 = GATE + 5 * one, 5 * one
        parts = [("w_qk", DC * HD, 2 * DC * HD, 0), ("w_qk", 0, DC * HD, 1), ("w_v", 0, DC * HD, 2),
                 ("w_o", 0, PAIRS * D, 3),
                 ("w_1", GATE + one, half_1, 6), ("w_1", half_1, GATE + NE * one, 6),
                 ("w_2", half_2, NE * one, 8)]
        ATTENTION_PARTS = 4
        pool_parts = [("w_1", 0, GATE + one, 5), ("w_2", 0, one, 7), ("w_2", one, half_2, 8)]

        x_tiles = x.rearrange("s (t p) d -> s p t d", p=P)
        out_tiles = out.rearrange("s (t p) d -> s p t d", p=P)

        block = ctx.enter_context(nc.Block())

        @block.sync
        def _(sp):
            sp.dma_start(x_next[:, :, :], x_tiles[0]).then_inc(xnext_loaded, 16)
            for k, (dst, src) in enumerate(loads):
                sp.dma_start(dst, src).then_inc(loaded[k], 16)
                if k == 3:
                    sp.dma_start(small2[:, :], b2_twice).then_inc(small_loaded, 16)
                    sp.dma_start(b1c[:, :, :], b1_cols).then_inc(small_loaded, 16)
                    sp.dma_start(sb2c[:, :], sb2_cols).then_inc(small_loaded, 16)
                    sp.dma_start(gate_b[:, :], gate_b_rows).then_inc(small_loaded, 16)
            sp.wait_ge(ring_full, 1)
            with sp.Fori(0, NSEQ) as i:
                sp.dma_start(x_next[:, :, :], x_tiles[(i + 1) % NSEQ]).then_inc(xnext_loaded, 16)
                sp.wait_ge(xnext_loaded, 16)
                sp.wait_ge(out_ready, i + 1)
                sp.dma_start(x_res[:, :, :], x_tiles[i]).then_inc(xres_loaded, 16)
                sp.wait_ge(out_ready, i + 2)
                sp.dma_start(out_tiles[i], x_next[:, :, :]).then_inc(stored, 16)
                stores = sp.to_reg(i * 16 + 16)
                sp.wait_ge(xnext_loaded, 16)
                sp.wait_ge(stored, stores)

        @block.gpsimd
        def _(pool):
            nc.gpsimd.memset(ident[:, :], 0.0)
            nc.gpsimd.memset(ones[:, :], 1.0)
            nc.gpsimd.memset(lower[:, :, :], 1.0)
            nc.gpsimd.memset(pick_f[:, :], 0.0).then_inc(const_ready, 1)
            pool.wait_ge(const_ready, 1)
            nc.gpsimd.affine_select(out=ident[:, :], in_=ident[:, :], compare_op=ALU.not_equal, fill=1.0,
                                    base=0, pattern=[[-1, P]], channel_multiplier=1)
            nc.gpsimd.affine_select(out=lower[:, :, :], in_=lower[:, :, :], compare_op=ALU.is_gt, fill=0.0,
                                    base=0, pattern=[[1, E], [-1, E]], channel_multiplier=0)
            nc.gpsimd.affine_select(out=pick_f[:, :], in_=pick_f[:, :], compare_op=ALU.not_equal,
                                    fill=1.0, base=0, pattern=[[-1, E]],
                                    channel_multiplier=1).then_inc(const_ready, 1)
            pool.wait_ge(const_ready, 2)
            nc.gpsimd.affine_select(out=pick_f[:, :], in_=pick_f[:, :], compare_op=ALU.not_equal,
                                    fill=1.0, base=-E, pattern=[[-1, E]],
                                    channel_multiplier=1).then_inc(const_ready, 1)

            for k, (name, a, b, load) in enumerate(pool_parts):
                if load == 5:
                    pool.wait_ge(loaded[4], 16)
                pool.wait_ge(loaded[load], 16)
                nc.gpsimd.tensor_copy(split[name][0][:, a:b], raw[name][:, a:b]).then_inc(pool_hi, 1)
                if k + 1 == len(pool_parts):
                    break
                pool.wait_ge(pool_hi, k + 1)
                nc.gpsimd.tensor_tensor(split[name][1][:, a:b], raw[name][:, a:b],
                                        split[name][0][:, a:b].bitcast(F32),
                                        ALU.subtract).then_inc(pool_lo, 1)
            with pool.Fori(0, NSEQ) as i:
                for p in range(PAIRS):
                    for u in range(3):
                        exps = pool.to_reg(i * 24 + (3 * p + u + 1))
                        pool.wait_ge(const_ready, 3)
                        pool.wait_ge(exp_done, exps)
                        for _, at in SCORE_UNITS[u]:
                            diag = prob(p, u)[:, :, at:at + P]
                            last = nc.gpsimd.affine_select(out=diag, in_=diag, compare_op=ALU.is_ge, fill=0.0,
                                                           base=0, pattern=[[0, 2], [1, P]],
                                                           channel_multiplier=-1)
                        last.then_inc(masked, 1)
                        if u == (2 if p == 0 else 1) and p + 1 < PAIRS:
                            pool.wait_ge(masked, i * 24 + 3 * p + 2)
                            if p >= 1:
                                pool.wait_ge(den_done, i * 8 + p)
                            t0, t13, t2 = prob(p, 0), prob(p, 1), prob(p, 2)
                            nc.gpsimd.tensor_tensor(key_sum[:, :, :], t0[:, :, P:N], t13[:, :, 0:N - P],
                                                    ALU.add).then_inc(sum_steps, 1)
                    if p in (0, PAIRS - 1):
                        continue
                    pool.wait_ge(masked, i * 24 + 3 * p + 3)
                    pool.wait_ge(sum_steps, i * SUMS + (3 * p - 1))
                    nc.gpsimd.tensor_tensor(key_sum[:, :, P:], key_sum[:, :, P:], t2[:, :, :],
                                            ALU.add).then_inc(sum_steps, 1)
                    pool.wait_ge(sum_steps, i * SUMS + 3 * p)
                    nc.gpsimd.tensor_tensor(key_sum[:, :, 2 * P:], key_sum[:, :, 2 * P:],
                                            t13[:, :, N - P:], ALU.add).then_inc(sum_steps, 1)

        @block.scalar
        def _(act):
            def split_hi(k):
                name, a, b, load = parts[k]
                act.wait_ge(loaded[load], 16)
                nc.scalar.copy(split[name][0][:, a:b], raw[name][:, a:b]).then_inc(hi_split, 1)

            def copy_xn_hi(slot, full):
                act.wait_ge(ring_full, full)
                nc.scalar.copy(xnT[0][:, :, :], slot[:, :, :]).then_inc(xn_hi, 1)

            def copy_v(slot, t, full):
                act.wait_ge(ring_full, full)
                nc.scalar.copy(v[:, t, :], slot[:, :, :].rearrange("p a n -> p (a n)")).then_inc(act_emptied, 1)

            def clamp(p, u, slot, full):
                act.wait_ge(ring_full, full)
                nc.scalar.activation(prob(p, u)[:, :, :], slot[:, :, 0:UNIT_COLS[u]],
                                     ACT.Tanh, scale=SCALE / SOFTCLAMP).then_inc(act_emptied, 1)

            def copy_k_hi(slot, pairs):
                act.wait_ge(k_projected, pairs)
                for h, r in enumerate(head_rows):
                    last = nc.scalar.copy(kT[r, h, :], slot[r, 1, :])
                last.then_inc(qk_hi, 1)

            def copy_q_hi(slot, full, his):
                act.wait_ge(ring_full, full)
                for h, r in enumerate(head_rows):
                    last = nc.scalar.copy(qT[r, h, :], slot[r, 0, :])
                last.then_inc(qk_hi, 1)
                act.wait_ge(qk_hi, his - 1)
                for h, r in enumerate(head_rows):
                    last = nc.scalar.copy(qT[head_rows[1 - h], h, :], qT[r, h, :].bitcast(F32))
                last.then_inc(qk_hi, 1)

            split_hi(0)
            split_hi(1)
            copy_xn_hi(ring[0], 1)
            split_hi(2)
            copy_k_hi(ring[1], 1)
            copy_q_hi(ring[1], 2, HI_FIRST)
            split_hi(3)
            for t in range(NT):
                copy_v(ring[t % 2], t, t + 3)
                if 1 <= t < NT - 1:
                    split_hi(ATTENTION_PARTS + t - 1)
            act.wait_ge(small_loaded, 16 * 4)
            act.wait_ge(gate_steps, 2)
            clamp(0, 0, ring[0], RING_FIRST - 1)
            split_hi(ATTENTION_PARTS + 2)
            clamp(0, 1, ring[1], RING_FIRST)
            act.wait_ge(act_emptied, ACT_FIRST - 1)
            nc.scalar.activation(prob(0, 0)[:, :, :], prob(0, 0)[:, :, :], ACT.Exp,
                                 scale=SOFTCLAMP).then_inc(exp_done, 1)
            with act.Fori(0, NSEQ) as i:
                def full(n):
                    return i * len(RING) + (RING_FIRST + n + 1)

                def exponentiate(n):
                    _, p, u = RING[n]
                    cols = prob(p, u)[:, :, :]
                    tanhs = emptied(n)[0] if n >= 0 else 0
                    act.wait_ge(act_emptied, i * ACT_TURN + (ACT_FIRST + tanhs))
                    nc.scalar.activation(cols, cols, ACT.Exp, scale=SOFTCLAMP).then_inc(exp_done, 1)

                waiting = -1
                for n, (kind, a, b) in enumerate(RING):
                    slot = ring[slot_index(n)]
                    if kind == "scores":
                        p, u = a, b
                        if u == 1 and p >= 1:
                            act.wait_ge(sum_steps, i * SUMS + (3 * p - 2))
                            if p == 1:
                                act.wait_ge(first_sums, i * 2 + 2)
                        if (p, u) == (0, 0):
                            nc.scalar.activation(table_call[:, :], ones[:, 0:1], ACT.Exp)
                            act.wait_ge(acc_done, i * 2 + 1)
                            nc.scalar.activation(yT[:, 0, :], acc[:, 0, :], ACT.Identity,
                                                 bias=sb2c[:, 0:1]).then_inc(y_copied[0], 1)
                        clamp(p, u, slot, full(n))
                        if waiting is not None:
                            exponentiate(waiting)
                        waiting = n
                    if kind == "turn1":
                        copy_xn_hi(slot, full(n))
                        exponentiate(waiting)
                        waiting = None
                    elif kind != "scores":
                        if kind == "qk" and a != 1:
                            copy_k_hi(slot, i * PAIRS + ((a or PAIRS) + 1))
                        if waiting is not None:
                            exponentiate(waiting)
                            waiting = None
                        if kind == "qk":
                            copy_q_hi(slot, full(n), i * HI_TURN + qk_his(a))
                    if kind == "attn":
                        act.wait_ge(attn_done, i * DC + 2)
                        nc.scalar.copy(attnT[:, 1, :], acc[:, 1, :]).then_inc(attn_copied[1], 1)
                    if kind == "v":
                        if a == 0:
                            act.wait_ge(o_steps, i * 32 + 4 * (PAIRS - 1))
                            act.wait_ge(last_values, i + 1)
                            nc.scalar.copy(norm[:, :], bank_o[:, :]).then_inc(out_copied, 1)
                        if a == NT - 1:
                            for k in range(2):
                                act.wait_ge(turned2, i * 2 + (k + 1))
                                nc.scalar.copy(*x2_half(0, k)).then_inc(x2_hi, 1)
                        copy_v(slot, a, full(n))
                        if a == NT - 1:
                            act.wait_ge(gate_steps, i * 12 + 4)
                            nc.scalar.activation(logit[:, :, :], logit[:, :, :], ACT.Exp).then_inc(gate_exp, 1)
                    if kind == "hidden":
                        e = a
                        act.wait_ge(ring_full, full(n))
                        if e >= 1:
                            act.wait_ge(h_steps, i * 26 + (3 * e - 1))
                        for c in range(FC):
                            last = nc.scalar.activation(gelu[:, c, :], slot[:, c, :], ACT.Gelu,
                                                        bias=b1c[:, e, c:c + 1])
                        last.then_inc(act_emptied, 1)
                assert waiting == len(RING) - 1

        @block.vector
        def _(dve):
            def split_lo(k):
                name, a, b, _ = parts[k]
                dve.wait_ge(hi_split, k + 1)
                nc.vector.tensor_tensor(split[name][1][:, a:b], raw[name][:, a:b],
                                        split[name][0][:, a:b].bitcast(F32),
                                        ALU.subtract).then_inc(lo_split, 1)

            def layernorm_stats(src):
                for t in range(NT):
                    last = nc.vector.bn_stats(stats[:, t, :], src[:, t, :])
                last.then_inc(ln_steps, 1)

            def layernorm_rstd(steps):
                layernorm_guess(steps)
                layernorm_newton(steps, range(NEWTON))

            def layernorm_guess(steps):
                stats_done = dve.to_reg(steps + 1)
                dve.wait_ge(xnext_loaded, 16)
                dve.wait_ge(ln_steps, stats_done)
                for t in range(NT):
                    last = nc.vector.bn_aggr(mean_var[:, t, :], stats[:, t, :])
                last.then_inc(ln_steps, 1)
                dve.wait_ge(ln_steps, steps + 2)
                nc.vector.tensor_scalar(var_eps[:, :, :], mean_var[:, :, 1:2], EPS, None, ALU.add)
                nc.vector.tensor_scalar(minus_half[:, :, :], mean_var[:, :, 1:2], EPS, -0.5, ALU.add,
                                        ALU.mult).then_inc(ln_steps, 1)
                dve.wait_ge(ln_steps, steps + 3)
                nc.vector.tensor_scalar(rstd[:, :, :].bitcast(I32), var_eps[:, :, :].bitcast(I32), -0.5,
                                        RSQRT_GUESS, ALU.mult, ALU.add).then_inc(ln_steps, 1)

            def layernorm_newton(steps, iterations):
                for k in iterations:
                    dve.wait_ge(ln_steps, steps + (4 + 3 * k))
                    nc.vector.tensor_tensor(newton[:, :, :], rstd[:, :, :], rstd[:, :, :],
                                            ALU.mult).then_inc(ln_steps, 1)
                    dve.wait_ge(ln_steps, steps + (5 + 3 * k))
                    nc.vector.tensor_tensor(newton[:, :, :], newton[:, :, :], minus_half[:, :, :],
                                            ALU.mult).then_inc(ln_steps, 1)
                    dve.wait_ge(ln_steps, steps + (6 + 3 * k))
                    nc.vector.scalar_tensor_tensor(rstd[:, :, :], newton[:, :, :], 1.5, rstd[:, :, :],
                                                   ALU.add, ALU.mult).then_inc(ln_steps, 1)

            def layernorm_apply(src, steps, half=None):
                dve.wait_ge(ln_steps, steps + LN_STEPS)
                for t in range(NT):
                    last = nc.vector.tensor_scalar(x_next[:, t, :], src[:, t, :], mean_var[:, t, 0:1],
                                                   rstd[:, t, :], ALU.subtract, ALU.mult)
                    if half is not None and t == NT // 2 - 1:
                        last.then_inc(half, 1)
                last.then_inc(xn_ready, 1)

            def empty_turned(slot, turns):
                dve.wait_ge(xn_hi, turns)
                nc.vector.tensor_tensor(xnT[1][:, :, :], slot[:, :, :], xnT[0][:, :, :].bitcast(F32),
                                        ALU.subtract).then_inc(dve_emptied, 1)

            def empty_qk(slot, his, first=None):
                lo_rows = head_rows[::-1]
                if first is None:
                    dve.wait_ge(qk_hi, his - 2)
                else:
                    pairs, turns = first
                    dve.wait_ge(k_projected, pairs)
                    for h, r in enumerate(head_rows):
                        last = nc.vector.tensor_copy(kT[r, h, :], slot[r, 1, :])
                    last.then_inc(k1_hi, 1)
                    dve.wait_ge(k1_hi, turns)
                for h, r in enumerate(head_rows):
                    last = nc.vector.tensor_tensor(kT[lo_rows[h], h, :], slot[r, 1, :],
                                                   kT[r, h, :].bitcast(F32), ALU.subtract)
                last.then_inc(k_lo, 1)
                dve.wait_ge(qk_hi, his - 1)
                for h, r in enumerate(head_rows):
                    last = nc.vector.tensor_tensor(q_lo[r, :], slot[r, 0, :], qT[r, h, :].bitcast(F32),
                                                   ALU.subtract)
                last.then_inc(dve_emptied, 1)

            dve.wait_ge(xnext_loaded, 16)
            layernorm_stats(x_next)
            layernorm_rstd(0)
            layernorm_apply(x_next, 0)
            split_lo(0)
            empty_turned(ring[0], 1)
            split_lo(1)
            split_lo(2)
            empty_qk(ring[1], HI_FIRST)
            split_lo(3)
            dve.wait_ge(const_ready, 3)
            nc.vector.tensor_copy(pick[:, :], pick_f[:, :]).then_inc(out_ready, 1)
            dve.wait_ge(small_loaded, 16 * 4)
            nc.vector.tensor_copy(b_2[0][:, :], small2[:, :]).then_inc(gate_steps, 1)
            dve.wait_ge(gate_steps, 1)
            nc.vector.tensor_tensor(b_2[1][:, :], small2[:, :], b_2[0][:, :].bitcast(F32),
                                    ALU.subtract).then_inc(gate_steps, 1)
            dve.wait_ge(gate_steps, 2)
            split_lo(ATTENTION_PARTS)
            split_lo(ATTENTION_PARTS + 1)
            split_lo(ATTENTION_PARTS + 2)
            name, a, b, _ = pool_parts[-1]
            dve.wait_ge(pool_hi, len(pool_parts))
            nc.vector.tensor_tensor(split[name][1][:, a:b], raw[name][:, a:b],
                                    split[name][0][:, a:b].bitcast(F32),
                                    ALU.subtract).then_inc(lo_split, 1)

            with dve.Fori(0, NSEQ) as i:
                def full(n):
                    return i * len(RING) + (RING_FIRST + n + 1)

                def normalise(p):
                    if p >= 1:
                        dve.wait_ge(o_steps, i * 32 + 4 * p)
                    dve.wait_ge(den_done, i * 8 + (p + 1))
                    if p + 1 < PAIRS:
                        nc.vector.reciprocal(norm[:, :], bank_d[:, :]).then_inc(o_steps, 1)
                        dve.wait_ge(o_steps, i * 32 + (4 * p + 1))
                        product = bank_o if p else acc[:, 0, :]
                    else:
                        nc.vector.reciprocal(last_recip[:, :, :],
                                             bank_d[:, 0:2 * NT].rearrange("p (t h) -> p t h", h=2)
                                             ).then_inc(o_steps, 1)
                        dve.wait_ge(last_spread, i + 1)
                        dve.wait_ge(out_copied, i + 1)
                        product = bank_d
                    nc.vector.tensor_tensor(norm[:, :], product[:, :], norm[:, :],
                                            ALU.mult).then_inc(o_steps, 1)

                def split_output(p):
                    dve.wait_ge(o_steps, i * 32 + (4 * p + 2))
                    if 1 <= p < PAIRS - 1:
                        dve.wait_ge(projected, i * (PAIRS - 1) + p)
                    hi, lo = oT if p < PAIRS - 1 else last_oT
                    nc.vector.tensor_copy(hi[:, :], norm[:, :]).then_inc(o_steps, 1)
                    dve.wait_ge(o_steps, i * 32 + (4 * p + 3))
                    nc.vector.tensor_tensor(lo[:, :], norm[:, :], hi[:, :].bitcast(F32),
                                            ALU.subtract).then_inc(o_steps, 1)

                next_ln = i * (2 * LN_STEPS) + LN_STEPS
                for p in range(PAIRS):
                    if p + 1 == PAIRS:
                        n = RING.index(("turn1", 0, 0))
                        empty_turned(ring[slot_index(n)], i + 2)
                    if p >= 1:
                        normalise(p - 1)
                    if p + 1 < PAIRS:
                        n = RING.index(("qk", p + 1, 0))
                        empty_qk(ring[slot_index(n)], i * HI_TURN + qk_his(p + 1),
                                 (i * PAIRS + 2, i + 1) if p == 0 else None)
                    else:
                        t0, t13, t2 = (prob(p, u) for u in range(3))
                        dve.wait_ge(masked, i * 24 + 23)
                        dve.wait_ge(den_done, i * PAIRS + p)
                        nc.vector.tensor_tensor(key_sum[:, :, :], t0[:, :, P:N], t13[:, :, 0:N - P],
                                                ALU.add).then_inc(last_sums, 1)
                        dve.wait_ge(last_sums, i * 3 + 1)
                        dve.wait_ge(masked, i * 24 + 24)
                        nc.vector.tensor_tensor(key_sum[:, :, P:], key_sum[:, :, P:], t2[:, :, :],
                                                ALU.add).then_inc(last_sums, 1)
                        dve.wait_ge(last_sums, i * 3 + 2)
                        nc.vector.tensor_tensor(key_sum[:, :, 2 * P:], key_sum[:, :, 2 * P:],
                                                t13[:, :, N - P:], ALU.add).then_inc(last_sums, 1)
                    if p == 0:
                        t13, t2 = prob(p, 1), prob(p, 2)
                        dve.wait_ge(masked, i * 24 + 3)
                        dve.wait_ge(sum_steps, i * SUMS + 1)
                        nc.vector.tensor_tensor(key_sum[:, :, P:], key_sum[:, :, P:], t2[:, :, :],
                                                ALU.add).then_inc(first_sums, 1)
                        dve.wait_ge(first_sums, i * 2 + 1)
                        nc.vector.tensor_tensor(key_sum[:, :, 2 * P:], key_sum[:, :, 2 * P:],
                                                t13[:, :, N - P:], ALU.add).then_inc(first_sums, 1)
                    if p >= 1:
                        split_output(p - 1)
                    if p == 1:
                        dve.wait_ge(xnext_loaded, i * 16 + 32)
                        layernorm_stats(x_next)
                    if p == 2:
                        layernorm_guess(next_ln)
                    if p == 3:
                        layernorm_newton(next_ln, range(2))
                    if p == 4:
                        layernorm_newton(next_ln, range(2, NEWTON))
                    if p == 5:
                        layernorm_apply(x_next, next_ln)
                normalise(PAIRS - 1)
                split_output(PAIRS - 1)

                dve.wait_ge(attn_done, i * DC + 1)
                nc.vector.tensor_copy(attnT[:, 0, :], acc[:, 0, :]).then_inc(attn_copied[0], 1)
                for k in range(2):
                    if k == 0:
                        dve.wait_ge(xres_loaded, i * 16 + 16)
                        dve.wait_ge(turned_attn, i + 1)
                    else:
                        dve.wait_ge(ring_full, full(ATTN))
                    half = x_res[:, 2 * k:2 * k + 2, :].rearrange("p t d -> p (t d)")
                    last = nc.vector.tensor_tensor(half, half, ring[slot_index(ATTN)][:, k, :], ALU.add)
                last.then_inc(dve_emptied, 1)
                dve.wait_ge(dve_emptied, i * DVE_TURN + (DVE_FIRST + emptied(ATTN)[1]))
                layernorm_stats(x_res)
                layernorm_rstd(next_ln + LN_STEPS)
                layernorm_apply(x_res, next_ln + LN_STEPS, xn_half)
                for k in range(2):
                    dve.wait_ge(x2_hi, i * 2 + (k + 1))
                    lo, turned = x2_half(1, k)
                    last = nc.vector.tensor_tensor(lo, turned, x2_half(0, k)[0].bitcast(F32),
                                                   ALU.subtract)
                last.then_inc(dve_emptied, 1)

                dve.wait_ge(gated, i + 1)
                nc.vector.tensor_scalar(gateT[:, :], bank_o[0:E, :], gate_b[:, :], None,
                                        ALU.add).then_inc(gate_copied, 1)
                gates = bank_d[:, 0:NT * E].rearrange("p (t e) -> p t e", t=NT)
                step = [0]

                def then(ins):
                    step[0] += 1
                    ins.then_inc(gate_steps, 1)
                    dve.wait_ge(gate_steps, i * 12 + (2 + step[0]))

                dve.wait_ge(turned_logits, i + 1)
                then(nc.vector.tensor_reduce(row1[:, :, :], gates, AX.X, ALU.max))
                then(nc.vector.tensor_tensor(logit[:, :, :], gates,
                                             row1[:, :, :].to_broadcast([P, NT, E]), ALU.subtract))
                dve.wait_ge(gate_exp, i + 1)
                then(nc.vector.tensor_reduce(row1[:, :, :], logit[:, :, :], AX.X, ALU.add))
                then(nc.vector.reciprocal(row1[:, :, :], row1[:, :, :]))
                then(nc.vector.tensor_tensor(prob8[:, :, :], logit[:, :, :],
                                             row1[:, :, :].to_broadcast([P, NT, E]), ALU.mult))
                shape = [P, NT, E, E]
                other = prob8[:, :, None, :].to_broadcast(shape)
                own = prob8[:, :, :, None].to_broadcast(shape)
                nc.vector.tensor_tensor(greater[:, :, :, :], other, own, ALU.is_gt)
                then(nc.vector.tensor_tensor(equal[:, :, :, :], other, own, ALU.is_equal))
                then(nc.vector.tensor_tensor(equal[:, :, :, :], equal[:, :, :, :],
                                             lower[:, None, :, :].to_broadcast(shape), ALU.mult))
                then(nc.vector.tensor_tensor(greater[:, :, :, :], greater[:, :, :, :], equal[:, :, :, :],
                                             ALU.add))
                then(nc.vector.tensor_reduce(combine[:, :, :], greater[:, :, :, :], AX.X, ALU.add))
                then(nc.vector.scalar_tensor_tensor(combine[:, :, :], combine[:, :, :], 2.0, prob8[:, :, :],
                                                    ALU.is_lt, ALU.mult))
                then(nc.vector.tensor_copy(combine2[:, :, 0:E], combine[:, :, :]))
                then(nc.vector.tensor_tensor(combine2[:, :, E:], combine[:, :, :],
                                             combine2[:, :, 0:E].bitcast(F32), ALU.subtract))
                assert step[0] == 12
                for e in range(NE):
                    n = RING.index(("hidden", e, 0))
                    dve.wait_ge(act_emptied, i * ACT_TURN + (ACT_FIRST + emptied(n)[0]))
                    if e == 1:
                        dve.wait_ge(turned_gate, i + 1)
                        nc.vector.tensor_copy(combineT[:, :], bank_d[0:2 * E, :]).then_inc(combine_ready, 1)
                    if e >= 1:
                        bank = bank_o if e % 2 else bank_d
                        dve.wait_ge(spread, i * 8 + e)
                        nc.vector.tensor_tensor(gelu[:, :, :], gelu[:, :, :],
                                                bank[:, None, :].to_broadcast([P, FC, N]),
                                                ALU.mult).then_inc(h_steps, 1)
                        dve.wait_ge(h_steps, i * 26 + 3 * e)
                    if e >= 2:
                        dve.wait_ge(y_done, i * 8 + (e - 1))
                    hh, hl = hT[e % 2]
                    nc.vector.tensor_copy(hh[:, :, :], gelu[:, :, :]).then_inc(h_steps, 1)
                    dve.wait_ge(h_steps, i * 26 + (3 * e + 1))
                    nc.vector.tensor_tensor(hl[:, :, :], gelu[:, :, :], hh[:, :, :].bitcast(F32),
                                            ALU.subtract).then_inc(h_steps, 1)

                n = RING.index(("qk", 0, 0))
                empty_qk(ring[slot_index(n)], i * HI_TURN + qk_his(0))
                dve.wait_ge(acc_done, i * 2 + 2)
                nc.vector.tensor_scalar(yT[:, 1, :], acc[:, 1, :], sb2c[:, 1:2], None,
                                        ALU.add).then_inc(y_copied[1], 1)
                for k, bank in enumerate((bank_o, bank_d)):
                    dve.wait_ge(turned_y, i * 2 + (k + 1))
                    half = slice(2 * k, 2 * k + 2)
                    last = nc.vector.tensor_tensor(x_next[:, half, :].rearrange("p t d -> p (t d)"),
                                                   x_res[:, half, :].rearrange("p t d -> p (t d)"),
                                                   bank[:, :], ALU.add)
                last.then_inc(out_ready, 1)

        @block.tensor
        def _(pe):
            def product(dsts, start, stop, lo_ready=None):
                for dst, terms in dsts:
                    for k, (w, m) in enumerate(terms):
                        pe.matmul(dst, w[0], m[0], start=start and k == 0, stop=False)
                        pe.matmul(dst, w[1], m[0], start=False, stop=False)
                if lo_ready is not None:
                    pe.wait_ge(*lo_ready)
                for dst, terms in dsts:
                    for k, (w, m) in enumerate(terms):
                        last = pe.matmul(dst, w[0], m[1], start=False, stop=stop and k == len(terms) - 1)
                return last

            def turn_tokens(slot, src):
                for c in range(DC):
                    for t in range(NT):
                        last = pe.transpose(slot[:, c, t * P:(t + 1) * P], src[:, t, c * P:(c + 1) * P],
                                            ident[:, :])
                last.then_inc(ring_full, 1)

            def project_qk(slot, p, tokens_lo=None, wq_ready=None):
                for m in (1, 0):
                    if m == 0 and wq_ready is not None:
                        pe.wait_ge(*wq_ready)
                    product([(slot[:, m, :], [([w[:, m, c, p * P:(p + 1) * P] for w in w_qk],
                                               [a[:, c, :] for a in xnT]) for c in range(DC)])],
                            True, True, tokens_lo if m else None
                            ).then_inc(k_projected if m else ring_full, 1)

            def project_v(slot, t, lo_ready=None, halves=range(2)):
                for k in halves:
                    for c in range(DC):
                        for w in w_v:
                            pe.matmul(slot[:, k, :], xnT[0][:, c, t * P:(t + 1) * P],
                                      w[:, c, k * N:(k + 1) * N], start=(c == 0 and w is w_v[0]),
                                      stop=False)
                if lo_ready is not None:
                    pe.wait_ge(*lo_ready)
                for k in halves:
                    for c in range(DC):
                        last = pe.matmul(slot[:, k, :], xnT[1][:, c, t * P:(t + 1) * P],
                                         w_v[0][:, c, k * N:(k + 1) * N], start=False, stop=c == DC - 1)
                return last

            def score_products(slot, u, q_lo_ready=None):
                tiles = [(slice(j * P, N), slice(j * P, (j + 1) * P), slice(at, at + N - j * P))
                         for j, at in SCORE_UNITS[u]]
                for k, (q, keys, to) in enumerate(tiles):
                    for h in range(2):
                        pe.matmul(slot[:, h, to], kT[:, h, keys], qT[:, h, q], start=k == 0, stop=False)
                if q_lo_ready is not None:
                    pe.wait_ge(*q_lo_ready)
                for k, (q, keys, to) in enumerate(tiles):
                    for h, r in enumerate(head_rows):
                        last = pe.matmul(slot[:, h, to], kT[r, h, keys], q_lo[r, q], start=False,
                                         stop=k == len(tiles) - 1)
                last.then_inc(ring_full, 1)

            pe.wait_ge(const_ready, 3)
            pe.wait_ge(xn_ready, 1)
            turn_tokens(ring[0], x_next)
            pe.wait_ge(lo_split, 1)
            pe.wait_ge(xn_hi, 1)
            project_qk(ring[1], 0, (dve_emptied, 1), (lo_split, 2))
            pe.wait_ge(lo_split, 3)
            for t in range(NT):
                if t == 1:
                    pe.wait_ge(dve_emptied, 2)
                elif t >= 2:
                    pe.wait_ge(act_emptied, t - 1)
                project_v(ring[t % 2], t).then_inc(ring_full, 1)
            pe.wait_ge(act_emptied, NT - 1)
            pe.wait_ge(k_lo, 1)
            pe.wait_ge(qk_hi, HI_FIRST)
            score_products(ring[0], 0)
            pe.wait_ge(act_emptied, NT)
            score_products(ring[1], 1)
            pe.wait_ge(lo_split, ATTENTION_PARTS)
            pe.wait_ge(gate_steps, 2)

            with pe.Fori(0, NSEQ) as i:
                def acts(k):
                    return i * ACT_TURN + (ACT_FIRST + k)

                def dves(k):
                    return i * DVE_TURN + (DVE_FIRST + k)

                turn = [0]

                def slot_for(*unit):
                    n = turn[0]
                    assert RING[n] == unit
                    turn[0] += 1
                    if n < 2:
                        pe.wait_ge(act_emptied, acts(n - 1))
                    elif RING[n - 2][0] in EMPTIED_BY_ACT:
                        pe.wait_ge(act_emptied, acts(emptied(n - 2)[0]))
                    else:
                        pe.wait_ge(dve_emptied, dves(emptied(n - 2)[1]))
                    return ring[slot_index(n)]

                def scores(p, u):
                    slot = slot_for("scores", p, u)
                    lo_ready = None
                    if u == 0:
                        n = RING.index(("qk", p, 0))
                        pe.wait_ge(k_lo, i * PAIRS + ((p or PAIRS) + 1))
                        pe.wait_ge(qk_hi, i * HI_TURN + qk_his(p))
                        lo_ready = (dve_emptied, dves(emptied(n)[1]))
                    score_products(slot, u, lo_ready)

                def values(p, us=range(3)):
                    if p == 0:
                        pe.wait_ge(out_ready, i + 1)
                    elif p >= 2 and us[0] == 0:
                        pe.wait_ge(o_steps, i * 32 + (4 * p - 2))
                    bank = acc[:, 0, :] if p == 0 else bank_o
                    units = [(u, j, at) for u in range(3) for j, at in SCORE_UNITS[u]]
                    for k, (u, j, at) in enumerate(units):
                        if u not in us:
                            continue
                        pe.wait_ge(masked, i * 24 + (3 * p + u + 1))
                        for h in range(2):
                            f = p * P + h * DH
                            last = pe.matmul(bank[h * DH:(h + 1) * DH, j * P:N], v[:, j, f:f + DH],
                                             prob(p, u)[:, h, at:at + N - j * P],
                                             start=(k == 0), stop=(k == len(units) - 1))
                    return last

                def denominators(p):
                    pe.wait_ge(sum_steps, i * SUMS + (3 * p + 1))
                    if p == 0:
                        pe.wait_ge(first_sums, i * 2 + 2)
                    for h in range(2):
                        pe.matmul(bank_d[h * DH:(h + 1) * DH, 0:P], ones[:, :],
                                  prob(p, 0)[:, h, 0:P], start=True, stop=True)
                    for h in range(2):
                        last = pe.matmul(bank_d[h * DH:(h + 1) * DH, P:N], ones[:, :], key_sum[:, h, :],
                                         start=True, stop=True)
                    last.then_inc(den_done, 1)

                def last_denominators():
                    p = PAIRS - 1
                    pe.wait_ge(last_sums, i * 3 + 3)
                    for t in range(NT):
                        for h in range(2):
                            sums = key_sum[:, h, (t - 1) * P:t * P] if t else prob(p, 0)[:, h, 0:P]
                            at = 2 * t + h
                            last = pe.matmul(bank_d[:, at:at + 1], sums, ones[:, 0:1], start=True, stop=True)
                    last.then_inc(den_done, 1)

                def spread_last():
                    pe.wait_ge(o_steps, i * 32 + (4 * (PAIRS - 1) + 1))
                    for t in range(NT):
                        for h in range(2):
                            last = pe.matmul(bank_d[h * DH:(h + 1) * DH, t * P:(t + 1) * P],
                                             last_recip[:, t, h:h + 1].to_broadcast([P, DH]),
                                             ident[:, :], start=True, stop=True)
                    last.then_inc(last_spread, 1)

                def project_out(p):
                    pe.wait_ge(o_steps, i * 32 + (4 * p + 3))
                    lo_ready = (o_steps, i * 32 + (4 * p + 4))
                    sums = [(acc[:, c, :], [([w[:, p, c * P:(c + 1) * P] for w in w_o],
                                             [a[:, :] for a in (oT if p < PAIRS - 1 else last_oT)])])
                            for c in range(DC)]
                    if p < PAIRS - 1:
                        product(sums, p == 0, False, lo_ready).then_inc(projected, 1)
                    else:
                        product(sums[:1], False, True, lo_ready).then_inc(attn_done, 1)
                        product(sums[1:], False, True).then_inc(attn_done, 1)

                def turn_back(src, copied, banks, done):
                    for c in range(DC):
                        pe.wait_ge(copied[c], i + 1)
                        for t in range(NT):
                            bank = banks[t // 2]
                            at = (t % 2) * D + c * P
                            last = pe.transpose(bank[:, at:at + P], src[:, c, t * P:(t + 1) * P], ident[:, :])
                            if c == DC - 1 and t % 2 == 1:
                                last.then_inc(done[t // 2], 1)

                for p in range(PAIRS - 1):
                    if p >= 1:
                        scores(p, 0)
                    if p >= 1:
                        scores(p, 1)
                    if p >= 1:
                        denominators(p - 1)
                    scores(p, 2)
                    project_qk(slot_for("qk", p + 1, 0), p + 1)
                    if p >= 2:
                        project_out(p - 2)
                    values(p)
                p = PAIRS - 1
                scores(p, 0)
                slot = slot_for("turn1", 0, 0)
                pe.wait_ge(xn_ready, i * 2 + 2)
                turn_tokens(slot, x_next)
                denominators(p - 1)
                scores(p, 1)
                scores(p, 2)
                project_out(p - 2)
                slot = slot_for("v", 0, 0)
                pe.wait_ge(xn_hi, i + 2)
                n = RING.index(("turn1", 0, 0))
                project_v(slot, 0, (dve_emptied, dves(emptied(n)[1]))).then_inc(ring_full, 1)
                values(p, [0, 1])
                last_denominators()
                values(p, [2]).then_inc(last_values, 1)
                spread_last()
                project_out(p - 1)
                project_out(p)
                slot = slot_for("attn", 0, 0)
                turn_back(attnT, attn_copied, [slot[:, 0, :], slot[:, 1, :]], [turned_attn, ring_full])
                project_v(slot_for("v", 1, 0), 1).then_inc(ring_full, 1)
                project_v(slot_for("v", 2, 0), 2).then_inc(ring_full, 1)
                slot_v3 = slot_for("v", 3, 0)
                project_v(slot_v3, 3, halves=[0])

                slot = slot_for("turn2", 0, 0)
                for k in range(2):
                    if k == 0:
                        pe.wait_ge(xn_half, i + 1)
                    else:
                        pe.wait_ge(xn_ready, i * 2 + 3)
                    for c in range(DC):
                        for t in range(2):
                            at = c * (N // 2) + t * P
                            last = pe.transpose(slot[:, k, at:at + P],
                                                x_next[:, 2 * k + t, c * P:(c + 1) * P], ident[:, :])
                    last.then_inc(turned2, 1)
                project_v(slot_v3, 3, halves=[1]).then_inc(ring_full, 2)
                pe.wait_ge(pool_lo, len(pool_parts) - 1)
                pe.wait_ge(lo_split, len(parts) + 1)
                pe.wait_ge(x2_hi, i * 2 + 2)
                n = RING.index(("turn2", 0, 0))
                product([(bank_o[:, :], [([w[:, c * E:c * E + P] for w in w_g],
                                          [a[:, c, :] for a in x2T]) for c in range(DC)])], True, True,
                        (dve_emptied, dves(emptied(n)[1]))).then_inc(gated, 1)

                def hidden_half(slot, e, f):
                    return product([(slot[:, f, :], [([w[:, e, c, f * P:(f + 1) * P] for w in w_1],
                                                      [a[:, c, :] for a in x2T]) for c in range(DC)])],
                                   True, True)

                def hidden(e):
                    slot = slot_for("hidden", e, 0)
                    for f in range(FC):
                        last = hidden_half(slot, e, f)
                    last.then_inc(ring_full, 1)

                def spread_weight(e):
                    bank = bank_o if e % 2 else bank_d
                    if e >= 3:
                        pe.wait_ge(h_steps, i * 26 + 3 * (e - 2))
                    pe.matmul(bank[:, :], pick[:, e - 1:e].to_broadcast([2 * E, P]), combineT[:, :], start=True,
                              stop=True).then_inc(spread, 1)

                def expert_out(e):
                    pe.wait_ge(h_steps, i * 26 + (3 * e + 1))
                    outs = [(acc[:, c, :], [([w[:, e, f, c * P:(c + 1) * P] for w in w_2],
                                             [a[:, f, :] for a in hT[e % 2]]) for f in range(FC)])
                            for c in range(DC)]
                    lo_ready = (h_steps, i * 26 + (3 * e + 2))
                    if e < NE - 1:
                        last = product(outs, e == 0, False, lo_ready)
                    else:
                        product(outs[:1], False, True, lo_ready).then_inc(acc_done, 1)
                        product(outs[1:], False, True).then_inc(acc_done, 1)
                    if e < NE - 1:
                        last.then_inc(y_done, 1)

                slot = slot_for("hidden", 0, 0)
                hidden_half(slot, 0, 0)
                copied = pe.to_reg(i + 1)
                pe.wait_ge(const_ready, 3)
                pe.wait_ge(gate_copied, copied)
                for t in range(NT):
                    last = pe.transpose(bank_d[:, t * E:(t + 1) * E], gateT[:, t * P:(t + 1) * P],
                                        ident[0:E, 0:E])
                last.then_inc(turned_logits, 1)
                for f in range(1, FC):
                    last = hidden_half(slot, 0, f)
                last.then_inc(ring_full, 1)
                hidden(1)
                hidden(2)
                pe.wait_ge(gate_steps, i * 12 + (2 + 12))
                for t in range(NT):
                    last = pe.transpose(bank_d[0:2 * E, t * P:(t + 1) * P], combine2[:, t, :].bitcast(F32),
                                        ident[:, :])
                last.then_inc(turned_gate, 1)
                expert_out(0)
                pe.wait_ge(combine_ready, i + 1)
                spread_weight(1)
                for c in range(DC):
                    for w in b_2:
                        pe.matmul(acc[:, c, :], w[:, c * P:(c + 1) * P], combineT[:, :], start=False,
                                  stop=False)
                for e in range(1, NE):
                    if e + 2 < NE:
                        hidden(e + 2)
                    if e + 1 < NE:
                        spread_weight(e + 1)
                    if e == NE - 2:
                        project_qk(slot_for("qk", 0, 0), 0)
                    expert_out(e)
                scores(0, 0)
                scores(0, 1)
                turn_back(yT, y_copied, [bank_o, bank_d], [turned_y, turned_y])
                assert turn[0] == len(RING)


_OUT = "out_dram"


def kernel(L0_attn_x, L0_attn_Wq, L0_attn_Wk, L0_attn_Wv, L0_attn_Wo, L0_ffn_gate_w, L0_ffn_gate_b,
           L0_ffn_sw1, L0_ffn_sb1, L0_ffn_sw2, L0_ffn_sb2, L0_ffn_w1, L0_ffn_b1, L0_ffn_w2, L0_ffn_b2):
    import numpy as np
    import concourse.bacc as bacc
    from concourse.bass_utils import run_bass_kernel_spmd

    def laid(a):
        return np.ascontiguousarray(a)

    b1 = np.concatenate([np.asarray(L0_ffn_sb1)[None], np.asarray(L0_ffn_b1)])
    arrays = {
        "x": laid(L0_attn_x),
        "wqT": laid(np.asarray(L0_attn_Wq).T),
        "wkT": laid(np.asarray(L0_attn_Wk).T),
        "wvT": laid(np.asarray(L0_attn_Wv).T),
        "woT": laid(np.asarray(L0_attn_Wo).T),
        "gate_w": laid(L0_ffn_gate_w),
        "gate_b_rows": laid(np.asarray(L0_ffn_gate_b).reshape(E, 1)),
        "w1s": laid(L0_ffn_sw1),
        "w1": laid(L0_ffn_w1),
        "w2s": laid(L0_ffn_sw2),
        "w2": laid(L0_ffn_w2),
        "b1_cols": laid(b1.reshape(NE, FC, P).transpose(2, 0, 1)),
        "b2_twice": laid(np.concatenate([np.asarray(L0_ffn_b2)] * 2)),
        "sb2_cols": laid(np.asarray(L0_ffn_sb2).reshape(DC, P).T),
    }
    nc = bacc.Bacc("TRN2", target_bir_lowering=False, num_devices=1)
    args = [nc.dram_tensor(f"in_{k}", a.shape, mybir.dt.from_np(a.dtype), kind="ExternalInput").ap()
            for k, a in arrays.items()]
    out = nc.dram_tensor(_OUT, (NSEQ, N, D), F32, kind="ExternalOutput").ap()
    block_program(nc, *args, out)
    r = run_bass_kernel_spmd(nc, [{f"in_{k}": a for k, a in arrays.items()}], core_ids=[0])
    return r.results[0][_OUT]
```
